# Optimizing a Trainium2 kernel written in Bass

```python
import numpy as np
import jax
import jax.numpy as jnp

def _softmax(x, axis=-1):
    return jax.nn.softmax(x, axis=axis)

def _gelu(x):
    return jax.nn.gelu(x, approximate=True)

def _silu(x):
    return jax.nn.silu(x)

def _sigmoid(x):
    return jax.nn.sigmoid(x)

def _layernorm(x, axis=-1, eps=1e-05):
    m = jnp.mean(x, axis=axis, keepdims=True)
    v = jnp.var(x, axis=axis, keepdims=True)
    return (x - m) / jnp.sqrt(v + eps)

def _scatter_add(tgt, idx, src, axis=0):
    return tgt.at[idx].add(src)

def _segment_sum(src, seg, n):
    return jax.ops.segment_sum(src, seg, n)
kernel_name = 'mk_xattn_ffn_d1_seqx_r2_d386d2'

def setup_inputs(seed: int=0):
    np.random.seed(seed)
    _w = jnp.asarray

    def _rec_inputs():
        import jax
        import jax.numpy as jnp
        _rk = jax.random.key(seed)
        x = -0.0003929 + 0.9999 * jax.random.normal(jax.random.fold_in(_rk, 1), (1, 4096, 512), jnp.float32)
        _lenS = 4096 - jax.random.randint(jax.random.fold_in(_rk, 7), (1,), 0, max(1, 4096 // 4) + 1, jnp.int32)
        _lenS2 = 3202 - jax.random.randint(jax.random.fold_in(_rk, 8), (1,), 0, max(1, 3202 // 4) + 1, jnp.int32)
        _ctx_2048P = jax.random.normal(jax.random.fold_in(_rk, 11), (1, 16, 1024), jnp.float32)
        _ctx_2048c = jax.random.dirichlet(jax.random.fold_in(_rk, 511), 0.3 * jnp.ones((16,), jnp.float32), (1, 3202))
        _ctx_2048t = jnp.einsum('bsk,bkd->bsd', _ctx_2048c, _ctx_2048P)
        _ctx_2048t = _ctx_2048t * jax.lax.rsqrt(jnp.mean(jnp.square(_ctx_2048t)) + 1e-12) * 0.953939
        ctx_2048 = 4.13588e-05 + 0.999923 * (_ctx_2048t + 0.3 * jax.random.normal(jax.random.fold_in(_rk, 611), (1, 3202, 1024), jnp.float32))
        _validS = jnp.arange(4096)[None, :] < _lenS[:, None]
        _validS2 = jnp.arange(3202)[None, :] < _lenS2[:, None]
        _causal = jnp.tril(jnp.ones((4096, 4096), dtype=bool))
        mask_BxS2_if0 = jnp.where(jnp.ones((1, 3202), dtype=bool), 4, 0).astype(jnp.int32)
        return (x, ctx_2048, mask_BxS2_if0)
    x, ctx_2048, mask_BxS2_if0 = _rec_inputs()

    def _L0_xattn_setup():
        import jax, jax.numpy as jnp
        import numpy as np
        B, L, P = (4, 2048, 512)
        D_MODEL = 512
        D_GLOBAL = 1024
        HEADDIM = 32
        EPSILON = 0.001
        RMS_EPS = 1e-05

        def rmsnorm(x, g, eps=RMS_EPS):
            var = jnp.mean(jnp.square(x), axis=-1, keepdims=True)
            return x * jax.lax.rsqrt(var + eps) * g

        def _hnet_depool(h, h_patch_full, patch_lens):
            h_patch = h_patch_full[..., :D_MODEL]
            bsz, plen = (h_patch.shape[0], h_patch.shape[1])
            seqlen = h.shape[1]
            logp = jnp.full((bsz, plen), -EPSILON, dtype=jnp.float32)
            bidx = jnp.cumsum(patch_lens, axis=1) - 1
            boundary_mask = jnp.zeros((bsz, seqlen), dtype=jnp.int32)
            boundary_mask = boundary_mask.at[jnp.arange(bsz)[:, None], bidx].set(1)
            dt = (-jnp.log(-jnp.expm1(logp))).astype(h_patch.dtype)
            x = h_patch / dt[..., None]
            n_heads = D_MODEL // HEADDIM
            A = -jnp.ones((n_heads,), dtype=jnp.float32)
            bcoef = jnp.exp(logp).astype(h_patch.dtype)
            x4 = x.reshape(bsz, plen, n_heads, HEADDIM)
            a = jnp.exp(dt[:, :, None] * A[None, None, :])
            u = (dt * bcoef)[:, :, None, None] * x4
            a_b = jnp.broadcast_to(a[..., None], u.shape)

            def comb(lft, rgt):
                aL, uL = lft
                aR, uR = rgt
                return (aL * aR, uL * aR + uR)
            _, s = jax.lax.associative_scan(comb, (a_b, u), axis=1)
            depool = s.reshape(bsz, plen, D_MODEL)
            plug = jnp.clip(jnp.cumsum(boundary_mask, axis=1) - 1, 0, plen - 1)
            depool_out = depool[jnp.arange(bsz)[:, None], plug]
            return depool_out + h
        key = jax.random.key(seed)
        k1, k2, k3, k4 = jax.random.split(key, 4)
        embeds = jax.random.normal(k1, (B, L, D_MODEL), dtype=jnp.float32)
        patch_embeds = jax.random.normal(k2, (B, P, D_GLOBAL), dtype=jnp.float32)
        patch_lens = jnp.full((B, P), L // P, dtype=jnp.int64)
        W_in = jax.random.normal(k3, (D_MODEL, D_MODEL), dtype=jnp.float32) * 0.02
        b_in = jnp.zeros((D_MODEL,), dtype=jnp.float32)
        g_res = jnp.ones((D_MODEL,), dtype=jnp.float32)
        g_init = jnp.ones((D_GLOBAL,), dtype=jnp.float32)
        return {'embeds': embeds, 'patch_embeds': patch_embeds, 'patch_lens': patch_lens, 'W_in': W_in, 'b_in': b_in, 'g_res': g_res, 'g_init': g_init}
    _L0_xattn_all = _L0_xattn_setup()
    _L0_xattn_in = {k: v for k, v in _L0_xattn_all.items() if k in ('W_in', 'b_in', 'g_res', 'g_init')}
    del _L0_xattn_all

    def _L0_ffn_setup():
        import jax, jax.numpy as jnp
        import numpy as np
        N_EMBD = 512
        N_STATE = 2048
        key = jax.random.key(seed)
        k_x, k_w1, k_b1, k_w2, k_b2 = jax.random.split(key, 5)
        x = jax.random.normal(k_x, (4, 1024, N_EMBD), dtype=jnp.float32)
        w1 = jax.random.normal(k_w1, (N_EMBD, N_STATE), dtype=jnp.float32) * (1.0 / np.sqrt(N_EMBD))
        b1 = jax.random.normal(k_b1, (N_STATE,), dtype=jnp.float32) * 0.02
        w2 = jax.random.normal(k_w2, (N_STATE, N_EMBD), dtype=jnp.float32) * (1.0 / np.sqrt(N_STATE))
        b2 = jax.random.normal(k_b2, (N_EMBD,), dtype=jnp.float32) * 0.02
        return {'x': x, 'w1': w1, 'b1': b1, 'w2': w2, 'b2': b2}
    _L0_ffn_all = _L0_ffn_setup()
    _L0_ffn_in = {k: v for k, v in _L0_ffn_all.items() if k in ('w1', 'b1', 'w2', 'b2')}
    del _L0_ffn_all
    return {'x': x, 'ctx_2048': ctx_2048, 'mask_BxS2_if0': mask_BxS2_if0, 'L0_xattn_W_in': _L0_xattn_in['W_in'], 'L0_xattn_b_in': _L0_xattn_in['b_in'], 'L0_xattn_g_res': _L0_xattn_in['g_res'], 'L0_xattn_g_init': _L0_xattn_in['g_init'], 'L0_ffn_w1': _L0_ffn_in['w1'], 'L0_ffn_b1': _L0_ffn_in['b1'], 'L0_ffn_w2': _L0_ffn_in['w2'], 'L0_ffn_b2': _L0_ffn_in['b2']}

def reference(x, ctx_2048, mask_BxS2_if0, L0_xattn_W_in, L0_xattn_b_in, L0_xattn_g_res, L0_xattn_g_init, L0_ffn_w1, L0_ffn_b1, L0_ffn_w2, L0_ffn_b2):
    import jax
    import jax.numpy as jnp

    def _L0_xattn_ref(embeds, patch_embeds, patch_lens, W_in, b_in, g_res, g_init):
        import jax, jax.numpy as jnp
        import numpy as np
        B, L, P = (4, 2048, 512)
        D_MODEL = 512
        D_GLOBAL = 1024
        HEADDIM = 32
        EPSILON = 0.001
        RMS_EPS = 1e-05

        def rmsnorm(x, g, eps=RMS_EPS):
            var = jnp.mean(jnp.square(x), axis=-1, keepdims=True)
            return x * jax.lax.rsqrt(var + eps) * g

        def _hnet_depool(h, h_patch_full, patch_lens):
            h_patch = h_patch_full[..., :D_MODEL]
            bsz, plen = (h_patch.shape[0], h_patch.shape[1])
            seqlen = h.shape[1]
            logp = jnp.full((bsz, plen), -EPSILON, dtype=jnp.float32)
            bidx = jnp.cumsum(patch_lens, axis=1) - 1
            boundary_mask = jnp.zeros((bsz, seqlen), dtype=jnp.int32)
            boundary_mask = boundary_mask.at[jnp.arange(bsz)[:, None], bidx].set(1)
            dt = (-jnp.log(-jnp.expm1(logp))).astype(h_patch.dtype)
            x = h_patch / dt[..., None]
            n_heads = D_MODEL // HEADDIM
            A = -jnp.ones((n_heads,), dtype=jnp.float32)
            bcoef = jnp.exp(logp).astype(h_patch.dtype)
            x4 = x.reshape(bsz, plen, n_heads, HEADDIM)
            a = jnp.exp(dt[:, :, None] * A[None, None, :])
            u = (dt * bcoef)[:, :, None, None] * x4
            a_b = jnp.broadcast_to(a[..., None], u.shape)

            def comb(lft, rgt):
                aL, uL = lft
                aR, uR = rgt
                return (aL * aR, uL * aR + uR)
            _, s = jax.lax.associative_scan(comb, (a_b, u), axis=1)
            depool = s.reshape(bsz, plen, D_MODEL)
            plug = jnp.clip(jnp.cumsum(boundary_mask, axis=1) - 1, 0, plen - 1)
            depool_out = depool[jnp.arange(bsz)[:, None], plug]
            return depool_out + h
        h = rmsnorm(embeds, g_res)
        h = jnp.einsum('bld,ed->ble', h, W_in) + b_in
        h_patch = rmsnorm(patch_embeds, g_init)
        return _hnet_depool(h, h_patch, patch_lens)

    def _L0_ffn_ref(x, w1, b1, w2, b2):
        import jax, jax.numpy as jnp
        import numpy as np
        N_EMBD = 512
        N_STATE = 2048
        h = jax.nn.gelu(jnp.einsum('bse,eh->bsh', x, w1) + b1, approximate=False)
        return jnp.einsum('bsh,he->bse', h, w2) + b2
    x = x + _L0_xattn_ref(_layernorm(x, axis=-1), ctx_2048, mask_BxS2_if0, L0_xattn_W_in, L0_xattn_b_in, L0_xattn_g_res, L0_xattn_g_init)
    x = x + _L0_ffn_ref(_layernorm(x, axis=-1), L0_ffn_w1, L0_ffn_b1, L0_ffn_w2, L0_ffn_b2)
    return x

_drawn_inputs = setup_inputs


def setup_inputs(seed=0):
    import zlib

    import numpy as np

    out = dict(_drawn_inputs(seed))
    spreads = {'L0_xattn_b_in': (0.0, 0.1), 'L0_xattn_g_res': (1.0, 0.2), 'L0_xattn_g_init': (1.0, 0.2)}
    factors = {'L0_ffn_b1': 6.752, 'L0_ffn_b2': 4.808}
    for name, (base, spread) in spreads.items():
        noise = np.random.default_rng([zlib.crc32(name.encode()), seed]).standard_normal(out[name].shape)
        drawn = base * np.exp(spread * noise) if base else spread * noise
        out[name] = jnp.asarray(drawn.astype(out[name].dtype))
    for name, factor in factors.items():
        out[name] = (out[name] * factor).astype(out[name].dtype)
    return out
```

```python
import math
from contextlib import ExitStack

import concourse.bass as bass
from concourse import mybir

ALU = mybir.AluOpType
ACT = mybir.ActivationFunctionType
F32 = mybir.dt.float32
F32R = mybir.dt.float32r
BF16 = mybir.dt.bfloat16
I32 = mybir.dt.int32
U32 = mybir.dt.uint32

P = 128
S, D, HID = 4096, 512, 2048
CTX, DG = 3202, 1024
TI = 4
GR = P * TI
NG = S // GR
NT = S // P
K = D // P
M = HID // P
PT = 8
NPAIR = NT // PT
R = 4
BLK = P * R
HIST = 16
HP = HIST // R
NB = 7
STEP = BLK - HIST
START1 = CTX - BLK - STEP * (NB - 2)
FIRST_ROWS = START1 + HIST
MJ = 26
WCH = 8
WC = 2048

LN_EPS = 1e-5
RMS_EPS = 1e-5
A = -math.expm1(-0.001)
B_COEF = math.exp(-0.001)

CREDIT = 2
ONE = 1


def wait_apart(engine, sem, value):
    engine.wait_ge(sem, value)
    engine.nop(nofuse=True)


class Tally:

    def __init__(self, sem):
        self.sem, self.n, self.base = sem, 0, 0

    def inc(self, ins):
        ins.then_inc(self.sem, 1)
        self.n += 1
        return self.base + self.n

    def looped(self, i, first, per):
        self.entered, self.per = self.n, per
        self.base = (i - first) * per

    def left(self, turns):
        assert self.n - self.entered == self.per, (self.n - self.entered, self.per)
        self.base = 0
        self.n = self.entered + turns * self.per


def xattn_ffn(nc, x, ctx, mask, w_in, b_in, g_res, g_init, w1, b1, w2, b2, out):
    x_v = x.rearrange("b (g p i) d -> (b g) p i d", p=P, i=TI)
    out_v = out.rearrange("b (g p i) d -> (b g) p i d", p=P, i=TI)
    ctx_v = ctx.rearrange("b s d -> (b s) d")
    mask_v = mask.rearrange("b s -> (b s)")
    w1_v = w1.rearrange("(k p) n -> k p n", p=P)
    w2_v = w2.rearrange("(c m p) n -> c p m n", m=4, p=P)
    win_v = w_in.rearrange("(c p) d -> p c d", p=P)
    x1_dram = nc.dram_tensor("x1_part", [NG, P, TI, D], F32, kind="Internal").ap()
    table = nc.dram_tensor("scan_table", [CTX, D], F32, kind="Internal").ap()

    es = ExitStack()
    with es:
        def sb(name, shape, dt=F32):
            return es.enter_context(nc.sbuf_tensor(name, shape, dt))

        def sem(name):
            return es.enter_context(nc.semaphore(name))

        HEAD = 2 * WCH * WC * 4
        KB = 1024
        SLAB = HEAD + (16 + 8 + 8 + 8 + 4 + 2 + 4 + 4 + 8 + 4 + 2 + 2) * KB
        slab = sb("slab", [P, SLAB // 4])
        at = [nc.sbuf_base - SLAB]

        def place(name, shape, dt=F32, size=0, offset=None):
            where = at[0] if offset is None else offset
            t = nc.alloc_sbuf_tensor_at(name, shape, dt, offset=where)
            if offset is None:
                at[0] += size
            return t

        w_hi_at = at[0]
        w_hi = place("w_hi", [P, WCH, WC], F32R, WCH * WC * 4)
        w_lo_at = at[0]
        w_lo = place("w_lo", [P, WCH, WC], F32R, WCH * WC * 4)
        w_raw = place("w_raw", [P, WCH, WC], F32, offset=w_lo_at)
        xt_at = at[0]
        xt_hi = place("xt_hi", [P, K, GR], F32R, 8 * KB)
        xt_lo = place("xt_lo", [P, K, GR], F32R, 8 * KB)
        win_hi = place("win_hi", [P, K, D], F32R, offset=xt_at)
        win_lo = place("win_lo", [P, K, D], F32R, offset=xt_at + 8 * KB)
        x_cur_at = at[0]
        x_cur = place("x_cur", [P, TI, D], F32, 8 * KB)
        x_next_at = at[0]
        x_next = place("x_next", [P, TI, D], F32, 8 * KB)
        n_rows = place("n_rows", [P, TI, D], F32, 8 * KB)
        dep = place("dep", [P, 2, D], F32, 4 * KB)
        g_f32 = place("g_f32", [P, D], F32, 2 * KB)
        h_hi = place("h_hi", [P, 2, GR], F32R, 4 * KB)
        h_lo = place("h_lo", [P, 2, GR], F32R, 4 * KB)
        cl = place("cl", [P, R, D], F32, 8 * KB)
        ch = place("ch", [P, 2, D], F32, 4 * KB)
        l3_hi = place("l3_hi", [P, D], F32R, 2 * KB)
        l3_lo = place("l3_lo", [P, D], F32R, 2 * KB)
        xa = place("xa", [P, PT, D], F32, offset=w_hi_at + 6 * WC * 4)
        oh_p = place("oh_p", [P, MJ, P], BF16, offset=w_hi_at + 5 * WC * 4)
        win_raw = place("win_raw", [P, K, D], F32, offset=w_hi_at + 4 * WC * 4)
        early_at = [x_next_at]

        def early(name, shape, dt=F32):
            t = place(name, shape, dt, offset=early_at[0])
            n = 2 if dt == BF16 else 4
            for v in shape[1:]:
                n *= v
            early_at[0] += -(-n // 32) * 32
            assert early_at[0] <= x_next_at + 8 * KB
            return t

        oh_q = early("oh_q", [P, MJ, NT], BF16)
        xb = place("xb", [P, 2, D], F32, offset=x_cur_at)
        na = place("na", [P, 2, D], F32, offset=x_cur_at + 4 * KB)

        b_in_b = sb("b_in_b", [P, D])
        b2_b = sb("b2_b", [P, D])
        g_init_b = sb("g_init_b", [P, D])
        ident = sb("ident", [P, P])
        tri = early("tri", [P, P])
        ones = early("ones", [P, P])
        band = early("band", [P, P])
        band_hi = sb("band_hi", [P, P], F32R)
        band_lo = sb("band_lo", [P, P], F32R)
        iota_p = early("iota_p", [P, P])
        b1_c = sb("b1_c", [P, M])
        g_res_c = sb("g_res_c", [P, K])
        neg_half = sb("neg_half", [P, TI])
        st_a = sb("st_a", [P, PT, 6])
        mv_a = sb("mv_a", [P, PT, 2])
        va_a = sb("va_a", [P, PT])
        ra = sb("ra", [P, PT])
        st_b = sb("st_b", [P, TI, 6])
        mv_b = sb("mv_b", [P, TI, 2])
        va_b = sb("va_b", [P, TI])
        rb = sb("rb", [P, TI])
        ss_h = sb("ss_h", [P, R])
        ss_l = sb("ss_l", [P, R])
        ss = sb("ss", [P, R])
        rc = sb("rc", [P, R])
        mask_i = early("mask_i", [P, MJ], I32)
        part_i = early("part_i", [P, 3, MJ], I32)
        part_f = early("part_f", [P, 3, MJ])
        cum_f = early("cum_f", [P, 3, MJ])
        one_row = early("one_row", [P, MJ])
        cum_i = early("cum_i", [P, 3, MJ], I32)
        ia = early("ia", [P, MJ], I32)
        ib = early("ib", [P, MJ], I32)
        ic = early("ic", [P, MJ], I32)
        fa = early("fa", [P, MJ])
        fb = early("fb", [P, MJ])
        pos_p = early("pos_p", [P, MJ])
        pos_q = early("pos_q", [P, MJ])
        cnt = early("cnt", [P, NG, TI])
        row_tot = early("row_tot", [P, NG])
        grp = early("grp", [P, NG])
        plug_f = early("plug_f", [P, NG, TI])
        plug = sb("plug", [P, NT], I32)
        idx = sb("idx", [P, TI], I32)

        def bank(name):
            return es.enter_context(nc.psum_tensor(name, [P, 512], F32))

        t_bank = [bank(f"t_bank{i}") for i in range(2)]
        h_bank = [bank(f"h_bank{i}") for i in range(2)]
        acc = [bank(f"acc{i}") for i in range(TI)]

        mask_loaded = sem("mask_loaded")
        win_loaded = sem("win_loaded")
        small_loaded = sem("small_loaded")
        xa_loaded = [sem(f"xa_loaded{i}") for i in range(PT)]
        xb_stored = [sem(f"xb_stored{i}") for i in range(2)]
        w_loaded = [sem(f"w_loaded{i}") for i in range(WCH)]
        cl_loaded = sem("cl_loaded")
        ch_loaded = [sem(f"ch_loaded{i}") for i in range(2)]
        table_stored = sem("table_stored")
        x_next_loaded = sem("x_next_loaded")
        gathered = [sem(f"gathered{i}") for i in range(2)]
        out_stored = sem("out_stored")
        consts_made = sem("consts_made")
        mask_cleared = sem("mask_cleared")
        tot_ready = sem("tot_ready")
        tot_summed = sem("tot_summed")
        onehots = sem("onehots")
        counted = sem("counted")
        cnt_ready = sem("cnt_ready")
        cnt_summed = sem("cnt_summed")
        plug_ready = sem("plug_ready")
        band_ready = sem("band_ready")
        win_t = sem("win_t")
        win_hi_done = sem("win_hi_done")
        win_lo_done = sem("win_lo_done")
        mv_a_ready = sem("mv_a_ready")
        ra_ready = sem("ra_ready")
        n_ready = sem("n_ready")
        t_done = sem("t_done")
        t_hi = sem("t_hi")
        t_lo = sem("t_lo")
        h_used = sem("h_used")
        acc_read = sem("acc_read")
        w_hi_done = sem("w_hi_done")
        w_lo_done = sem("w_lo_done")
        w_late = sem("w_late")
        sq_done = sem("sq_done")
        rc_ready = sem("rc_ready")
        scaled = sem("scaled")
        l3_ready = sem("l3_ready")
        carried = sem("carried")
        block_ready = sem("block_ready")
        idx_ready = sem("idx_ready")
        x1_ready = sem("x1_ready")
        mv_b_ready = sem("mv_b_ready")
        rb_ready = sem("rb_ready")
        x_cur_ready = sem("x_cur_ready")
        ffn1_done = sem("ffn1_done")
        gelu_done = sem("gelu_done")
        h_split = sem("h_split")
        act_self = sem("act_self")
        dve_self = sem("dve_self")
        pool_self = sem("pool_self")

        block = es.enter_context(nc.Block())

        def block_start(b):
            return START1 + STEP * (b - 1)

        @block.sync
        def _(sp):
            wait_apart(sp, mask_cleared, 1)
            full = CTX // MJ
            sp.dma_start(mask_i[0:full, :], mask_v[0:full * MJ].rearrange("(p j) -> p j", j=MJ)).then_inc(mask_loaded, 16)
            sp.dma_start(mask_i[full:full + 1, 0:CTX - full * MJ],
                         mask_v[full * MJ:CTX].rearrange("(p j) -> p j", p=1)).then_inc(mask_loaded, 16)
            sp.dma_start(xa[:, 0, :], x_v[0, :, 0, :]).then_inc(xa_loaded[0], 16)
            sp.dma_start(win_raw[:], win_v).then_inc(win_loaded, 16)
            for t in range(1, PT - 1):
                sp.dma_start(xa[:, t, :], x_v[t // TI, :, t % TI, :]).then_inc(xa_loaded[t], 16)

            def load_low_half(b, first_row):
                if not isinstance(b, int) or b >= 1:
                    wait_apart(sp, table_stored, 16 * b + 16)
                rows = ctx_v[bass.ds(first_row, BLK), :].rearrange("(p j) d -> p j d", j=R)
                sp.dma_start(cl[:], rows[:, :, 0:D]).then_inc(cl_loaded, 16)

            def load_high_half(b, first_row, j):
                if j >= 2:
                    wait_apart(sp, sq_done, R * b + j - 1)
                rows = ctx_v[bass.ds(first_row, BLK), :].rearrange("(p j) d -> p j d", j=R)
                sp.dma_start(ch[:, j % 2, :], rows[:, j, D:DG]).then_inc(ch_loaded[j % 2], 16)

            def store_block(b, first_row):
                wait_apart(sp, block_ready, b + 1)
                if isinstance(b, int) and b == 0:
                    whole = FIRST_ROWS // R
                    sp.dma_start(table[0:whole * R, :].rearrange("(p j) d -> p j d", j=R),
                                 cl[0:whole, :, :]).then_inc(table_stored, 16)
                    sp.dma_start(table[whole * R:FIRST_ROWS, :].rearrange("(p j) d -> p j d", p=1),
                                 cl[whole:whole + 1, 0:FIRST_ROWS - whole * R, :]).then_inc(table_stored, 16)
                else:
                    sp.dma_start(table[bass.ds(first_row + HIST, STEP), :].rearrange("(p j) d -> p j d", j=R),
                                 cl[HP:P, :, :]).then_inc(table_stored, 16)

            def pair(h, first_row, last=False):
                for t in range(PT):
                    n = PT * h + t
                    if t == 0:
                        load_low_half(h, first_row)
                        load_high_half(h, first_row, 0)
                        load_high_half(h, first_row, 1)
                    if t in (1, 2):
                        load_high_half(h, first_row, t + 1)
                    if not (isinstance(h, int) and n == 0):
                        wait_apart(sp, acc_read, n)
                        v = (t - 1) % PT
                        g = 2 * h + (t - 1) // TI
                        sp.dma_start(x1_dram[g, :, v % TI, :], xb[:, v % 2, :]).then_inc(xb_stored[v % 2], 16)
                    if not last or t == 0:
                        u = (t + PT - 1) % PT
                        g = 2 * h + (t + PT - 1) // TI
                        sp.dma_start(xa[:, u, :], x_v[g, :, u % TI, :]).then_inc(xa_loaded[u], 16)
                    if t == PT - 1:
                        store_block(h, first_row)
                    if last and t == 0:
                        wait_apart(sp, xb_stored[0], 16 * 2)
                        wait_apart(sp, xb_stored[1], 16 * 2)
                        wait_apart(sp, plug_ready, 1)
                        wait_apart(sp, band_ready, 1)
                        sp.dma_start(x_next[:], x1_dram[0, :, :, :]).then_inc(x_next_loaded, 16)

            pair(0, 0)
            with sp.Fori(1, NPAIR - 1) as h:
                pair(h, block_start(h))
            pair(NPAIR - 1, block_start(NPAIR - 1), last=True)
            wait_apart(sp, acc_read, NT)
            sp.dma_start(x1_dram[NG - 1, :, TI - 1, :], xb[:, 1, :]).then_inc(xb_stored[1], 16)
            for s in xb_stored:
                wait_apart(sp, s, 16 * NT // 2)

            def group(g, scan, prep):
                if prep:
                    wait_apart(sp, x_cur_ready, g + 1)
                    sp.dma_start(x_next[:], x1_dram[g + 1, :, :, :]).then_inc(x_next_loaded, 16)
                if scan:
                    b = NPAIR + g
                    first_row = block_start(b)
                    load_low_half(b, first_row)
                    for j in range(R):
                        load_high_half(b, first_row, j)
                    store_block(b, first_row)
                for i in range(TI):
                    wait_apart(sp, acc_read, NT + TI * g + i + 1)
                    sp.dma_start(out_v[g, :, i, :], x_cur[:, i, :]).then_inc(out_stored, 16)

            with sp.Fori(0, NB - NPAIR) as g:
                group(g, True, True)
            with sp.Fori(NB - NPAIR, NG - 1) as g:
                group(g, False, True)
            group(NG - 1, False, False)
            wait_apart(sp, out_stored, 16 * TI * NG)
            wait_apart(sp, table_stored, 16 * (NB + 1))

        @block.gpsimd
        def _(pool):
            own = Tally(pool_self)

            def step(ins):
                wait_apart(pool, pool_self, own.inc(ins))

            pool.memset(ident[:], 0.0).then_inc(pool_self, 1)
            pool.memset(tri[:], 1.0).then_inc(pool_self, 1)
            pool.memset(band[:], 0.0).then_inc(pool_self, 1)
            own.n = 3
            pool.wait_ge(pool_self, 3)
            pool.affine_select(out=ident[:], in_=ident[:], compare_op=ALU.not_equal, fill=1.0, base=0,
                               pattern=[[-1, P]], channel_multiplier=1).then_inc(consts_made, 1)
            pool.affine_select(out=tri[:], in_=tri[:], compare_op=ALU.is_gt, fill=0.0, base=0,
                               pattern=[[1, P]], channel_multiplier=-1).then_inc(consts_made, 1)
            pool.memset(ones[:], 1.0).then_inc(consts_made, 1)
            pool.iota(iota_p[:], [[1, P]], base=0, channel_multiplier=0,
                      allow_small_or_imprecise_dtypes=True).then_inc(consts_made, 1)
            pool.memset(neg_half[:], -0.5).then_inc(pool_self, 1)
            own.n += 1
            for q in range(HP):
                step(pool.affine_select(out=band[:], in_=band[:], compare_op=ALU.not_equal, fill=A ** (R * q),
                                        base=q + 1, pattern=[[-1, P]], channel_multiplier=1))
            pool.sem_inc(consts_made, 1)

            def tile_scale(n, t):
                wait_apart(pool, mv_a_ready, n + 1)
                step(pool.tensor_scalar(va_a[:, t:t + 1], mv_a[:, t, 1:2], 1.0 + RMS_EPS, LN_EPS * RMS_EPS,
                                        ALU.mult, ALU.add))
                pool.tensor_tensor(ra[:, t:t + 1], va_a[:, t:t + 1], neg_half[:, 0:1], ALU.pow).then_inc(ra_ready, 1)

            def low_weights(c):
                pool.wait_ge(w_hi_done, c + 1)
                pool.tensor_tensor(w_lo[:, c, :], w_raw[:, c, :], w_hi[:, c, :].bitcast(F32),
                                   ALU.subtract).then_inc(w_lo_done, 1)

            def context_scale(b):
                pool.wait_ge(sq_done, R * b + R)
                step(pool.tensor_tensor(ss[:], ss_h[:], ss_l[:], ALU.add))
                step(pool.tensor_scalar(ss[:], ss[:], 1.0 / DG, RMS_EPS, ALU.mult, ALU.add))
                step(pool.tensor_tensor(rc[:], ss[:], neg_half[:], ALU.pow))
                pool.tensor_scalar(rc[:], rc[:], B_COEF, 1.0, ALU.mult, ALU.mult).then_inc(rc_ready, 1)

            def gather_indices(g):
                step(pool.tensor_copy(idx[:], plug[:, bass.ds(TI * g, TI)]))

            def gather(g, i, blocks):
                wait_apart(pool, table_stored, 16 * (blocks + 1))
                rows = table[0:block_start(blocks - 1) + BLK, :]
                pool.indirect_dma_start(dep[:, i % 2, :], None, rows, bass.IndirectOffsetOnAxis(
                    ap=idx[:, i:i + 1].bitcast(U32), axis=0)).then_inc(gathered[i % 2], 16)

            def add_context(g, i):
                pool.wait_ge(gathered[i % 2], 16 * (2 * g + i // 2 + 1))
                step(pool.tensor_tensor(dep[:, i % 2, :], dep[:, i % 2, :], g_init_b[:], ALU.mult))
                step(pool.tensor_tensor(dep[:, i % 2, :], dep[:, i % 2, :], b_in_b[:], ALU.add))
                ins = pool.tensor_tensor(x_next[:, i, :], x_next[:, i, :], dep[:, i % 2, :], ALU.add)
                ins.then_inc(x1_ready, 1)
                wait_apart(pool, x1_ready, TI * g + i + 1)

            def group_scale(g):
                wait_apart(pool, mv_b_ready, TI * (g + 1))
                step(pool.tensor_scalar(va_b[:], mv_b[:, :, 1], LN_EPS, 1.0, ALU.add, ALU.mult))
                pool.tensor_tensor(rb[:], va_b[:], neg_half[:], ALU.pow).then_inc(rb_ready, 1)

            def prepare(g, blocks):
                gather_indices(g)
                for i in range(2):
                    gather(g, i, blocks)
                pool.wait_ge(x_next_loaded, 16 * (g + 1))
                for i in range(TI):
                    add_context(g, i)
                    if i < 2:
                        gather(g, i + 2, blocks)

            def pair(h, last=False):
                for t in range(PT):
                    n = PT * h + t
                    if not last or t + 2 < PT:
                        tile_scale(n + 2, (t + 2) % PT)
                    if t == 3 and not last:
                        low_weights(2 * h)
                    if t == 6 and not last:
                        low_weights(2 * h + 1)
                    if t == 4:
                        context_scale(h)
                    if last and t == 1:
                        pool.wait_ge(small_loaded, 16 * 5)
                        pool.wait_ge(plug_ready, 1)
                        gather_indices(0)
                        for i in (0, 1):
                            gather(0, i, 3)
                    if last and t in (3, 5):
                        if t == 3:
                            pool.wait_ge(x_next_loaded, 16)
                        for i in (t - 3, t - 2):
                            add_context(0, i)
                            if t == 3:
                                gather(0, i + 2, 3)
                if last:
                    group_scale(0)

            tile_scale(0, 0)
            tile_scale(1, 1)
            pair(0)
            with pool.Fori(1, NPAIR - 1) as h:
                own.looped(h, 1, 16 // 2 + 3)
                pair(h)
            own.left(NPAIR - 2)
            pair(NPAIR - 1, last=True)
            pool.wait_ge(acc_read, NT)
            for c in (6, 7):
                pool.wait_ge(w_loaded[c], 16)
                step(pool.tensor_copy(w_hi[:, c, :], w_raw[:, c, :]))
                pool.tensor_tensor(w_lo[:, c, :], w_raw[:, c, :], w_hi[:, c, :].bitcast(F32),
                                   ALU.subtract).then_inc(w_late, 1)

            for s in xb_stored:
                pool.wait_ge(s, 16 * NT // 2)

            def group(g, scan, prep):
                pool.wait_ge(n_ready, NT + TI * (g + 1))
                if not isinstance(g, int) or g > 0:
                    pool.wait_ge(out_stored, 16 * TI * g)
                pool.tensor_tensor(x_cur[:], x_next[:], b2_b[:].unsqueeze(1).to_broadcast([P, TI, D]),
                                   ALU.add).then_inc(x_cur_ready, 1)
                if scan:
                    context_scale(NPAIR + g)
                if prep:
                    prepare(g + 1, g + 3 if scan else NB)
                    group_scale(g + 1)

            for g in range(NB - NPAIR):
                group(g, True, True)
            with pool.Fori(NB - NPAIR, NG - 1) as g:
                own.looped(g, NB - NPAIR, 1 + 2 * TI + 1)
                group(g, False, True)
            own.left(NG - 1 - (NB - NPAIR))
            group(NG - 1, False, False)

        @block.scalar
        def _(act):
            own = Tally(act_self)
            act.dma_start(g_res_c[:], g_res.rearrange("(k p) -> p k", p=P),
                          allow_slow_non_contiguous=True).then_inc(small_loaded, 16)
            for c in range(WCH):
                v = w_raw[:, c, :]
                if c < 4:
                    act.dma_start(v, w1_v[c, :, :]).then_inc(w_loaded[c], 16)
                else:
                    act.dma_start(v.rearrange("p (m n) -> p m n", m=4), w2_v[c - 4, :, :, :]).then_inc(w_loaded[c], 16)
                if c == 0:
                    act.dma_start(b1_c[:], b1.rearrange("(m p) -> p m", p=P),
                                  allow_slow_non_contiguous=True).then_inc(small_loaded, 16)
                    for v, src in ((b_in_b, b_in), (b2_b, b2), (g_init_b, g_init[0:D])):
                        act.dma_start(v[:], src.rearrange("(a n) -> a n", a=1).to_broadcast([P, D]))\
                           .then_inc(small_loaded, 16)
            act.wait_ge(small_loaded, 16 * 5)
            for k in range(K):
                act.wait_ge(win_t, k + 1)
                act.activation(win_hi[:, k, :], acc[k][:], ACT.Copy, scale=g_res_c[:, k:k + 1]).then_inc(win_hi_done, 1)

            def tile_high(n, t):
                act.wait_ge(t_done, n + 1)
                if not isinstance(n, int) or n >= 2:
                    act.wait_ge(h_used, n - 1)
                act.activation(h_hi[:, t % 2, :], t_bank[t % 2][:], ACT.Copy).then_inc(t_hi, 1)

            def squares(b, j):
                act.wait_ge(ch_loaded[j % 2], 16 * (2 * b + j // 2 + 1))
                v = own.inc(act.activation(ch[:, j % 2, :], ch[:, j % 2, :], ACT.Square, accum_out=ss_h[:, j:j + 1]))
                act.wait_ge(act_self, v)
                if j == 0:
                    act.wait_ge(cl_loaded, 16 * (b + 1))
                act.activation(ch[:, j % 2, :], cl[:, j, :], ACT.Square, accum_out=ss_l[:, j:j + 1]).then_inc(sq_done, 1)

            def scale_rows(b):
                act.wait_ge(rc_ready, b + 1)
                for j in range(R):
                    act.activation(cl[:, j, :], cl[:, j, :], ACT.Copy, scale=rc[:, j:j + 1]).then_inc(scaled, 1)

            def pair(h, last=False):
                for t in range(PT):
                    n = PT * h + t
                    tile_high(n, t)
                    if t < R:
                        squares(h, t)
                    if t == 5:
                        scale_rows(h)
                    if t in (2, 5) and not last:
                        half = t // 4
                        if not isinstance(h, int):
                            act.wait_ge(counted, 1)
                        act.wait_ge(w_lo_done, 2 * h + half) if not isinstance(h, int) else None
                        c = 2 * h + half
                        if isinstance(h, int):
                            act.wait_ge(w_loaded[c], 16)
                        act.activation(w_hi[:, c, :], w_raw[:, c, :], ACT.Copy).then_inc(w_hi_done, 1)

            pair(0)
            for c in range(2, 6):
                act.wait_ge(w_loaded[c], 16)
            with act.Fori(1, NPAIR - 1) as h:
                own.looped(h, 1, R)
                pair(h)
            own.left(NPAIR - 2)
            pair(NPAIR - 1, last=True)
            act.sem_inc(gelu_done, CREDIT)

            def transposed_high(g, i):
                act.wait_ge(t_done, NT + TI * g + i + 1)
                act.activation(xt_hi[:, :, i * P:(i + 1) * P], t_bank[i % 2][:].rearrange("p (k r) -> p k r", k=K),
                               ACT.Copy).then_inc(t_hi, 1)

            act.wait_ge(h_used, NT)
            for i in range(TI):
                transposed_high(0, i)

            def group(g, scan, prep):
                for m in range(M):
                    act.wait_ge(ffn1_done, M * g + m + 1)
                    act.wait_ge(h_used, NT + M * g + m - 1)
                    act.activation(h_hi[:, m % 2, :], h_bank[m % 2][:], ACT.Gelu, bias=b1_c[:, m:m + 1])
                    act.wait_ge(h_split, ONE + M * g + m)
                    act.activation(g_f32[:], h_bank[m % 2][:], ACT.Gelu, bias=b1_c[:, m:m + 1]).then_inc(gelu_done, 1)
                    if scan and 1 <= m <= R:
                        squares(NPAIR + g, m - 1)
                    if scan and m == 7:
                        scale_rows(NPAIR + g)
                if prep:
                    for i in range(TI):
                        transposed_high(g + 1, i)

            with act.Fori(0, NB - NPAIR) as g:
                own.looped(g, 0, R)
                group(g, True, True)
            own.left(NB - NPAIR)
            with act.Fori(NB - NPAIR, NG - 1) as g:
                group(g, False, True)
            group(NG - 1, False, False)

        @block.tensor
        def _(pe):
            pe.wait_ge(consts_made, 4)
            pe.wait_ge(tot_ready, 1)
            nc.tensor.matmul(h_bank[1][:, 0:3], tri[:], part_f[:, :, 0], start=True, stop=True).then_inc(tot_summed, 1)
            pe.wait_ge(win_loaded, 16)
            for k in range(K):
                for c in range(K):
                    ins = nc.tensor.transpose(acc[k][:, c * P:(c + 1) * P], win_raw[:, c, k * P:(k + 1) * P], ident[:])
                ins.then_inc(win_t, 1)

            def transpose_first(n, t):
                pe.wait_ge(n_ready, n + 1)
                if not isinstance(n, int) or n >= 2:
                    pe.wait_ge(t_lo, n - 1)
                for k in range(K):
                    ins = nc.tensor.transpose(t_bank[t % 2][:, k * P:(k + 1) * P], na[:, t % 2, k * P:(k + 1) * P], ident[:])
                ins.then_inc(t_done, 1)

            def split_product(dst, a_hi, a_lo, b_hi, b_lo, first, final):
                nc.tensor.matmul(dst, a_hi, b_hi, start=first, stop=False)
                nc.tensor.matmul(dst, a_hi, b_lo, start=False, stop=False)
                return nc.tensor.matmul(dst, a_lo, b_hi, start=False, stop=final)

            def project(n, t):
                pe.wait_ge(t_lo, n + 1)
                if not isinstance(n, int) or n >= TI:
                    pe.wait_ge(acc_read, n - TI + 1)
                for k in range(K):
                    c = slice(k * P, (k + 1) * P)
                    ins = split_product(acc[t % TI][:], h_hi[:, t % 2, c], h_lo[:, t % 2, c],
                                        win_hi[:, k, :], win_lo[:, k, :], k == 0, k == K - 1)
                ins.then_inc(h_used, 1)

            def carry(b, dst):
                pe.wait_ge(l3_ready, b + 1)
                split_product(dst, band_hi[:], band_lo[:], l3_hi[:], l3_lo[:], True, True).then_inc(carried, 1)

            transpose_first(0, 0)
            pe.wait_ge(onehots, 1)
            for j in range(MJ):
                ins = nc.tensor.matmul(h_bank[0][:, 0:NT], oh_p[:, j, :], oh_q[:, j, :], start=(j == 0), stop=(j == MJ - 1))
            ins.then_inc(counted, 1)
            pe.wait_ge(cnt_ready, 1)
            nc.tensor.matmul(h_bank[1][:, 0:NG], tri[:], row_tot[:], start=True, stop=True)
            nc.tensor.matmul(h_bank[1][:, 64:64 + NG], ones[:], row_tot[:], start=True, stop=True).then_inc(cnt_summed, 1)
            pe.wait_ge(win_lo_done, K)
            pe.wait_ge(win_hi_done, K)
            pe.wait_ge(band_ready, 1)

            def transpose_second(g, i):
                pe.wait_ge(n_ready, NT + TI * g + i + 1)
                pe.wait_ge(t_lo, NT + TI * g + i - 1)
                for k in range(K):
                    ins = nc.tensor.transpose(t_bank[i % 2][:, k * P:(k + 1) * P], n_rows[:, i, k * P:(k + 1) * P], ident[:])
                ins.then_inc(t_done, 1)

            def pair(h, last=False):
                for t in range(PT):
                    n = PT * h + t
                    if not last or t + 1 < PT:
                        transpose_first(n + 1, (t + 1) % PT)
                    project(n, t)
                    if t == 6:
                        carry(h, h_bank[0][:])

            pair(0)
            with pe.Fori(1, NPAIR - 1) as h:
                pair(h)
            pair(NPAIR - 1, last=True)
            for i in range(TI):
                transpose_second(0, i)

            pe.wait_ge(w_lo_done, 6)
            pe.wait_ge(w_hi_done, 6)

            def ffn1(g, m):
                pe.wait_ge(gelu_done, M * g + m + 1)
                if m == 0:
                    pe.wait_ge(t_hi, NT + TI * (g + 1))
                    pe.wait_ge(t_lo, NT + TI * (g + 1))
                for k in range(K):
                    c = slice(m * P, (m + 1) * P)
                    ins = split_product(h_bank[m % 2][:], w_hi[:, k, c], w_lo[:, k, c], xt_hi[:, k, :], xt_lo[:, k, :],
                                        k == 0, k == K - 1)
                ins.then_inc(ffn1_done, 1)

            def ffn2(g, m):
                pe.wait_ge(h_split, ONE + M * g + m + 1)
                if m == 0:
                    pe.wait_ge(acc_read, NT + TI * g)
                if m == 8:
                    pe.wait_ge(w_late, 2)
                c, r = 4 + m // 4, slice((m % 4) * D, (m % 4 + 1) * D)
                for i in range(TI):
                    s = slice(i * P, (i + 1) * P)
                    ins = split_product(acc[i][:], h_hi[:, m % 2, s], h_lo[:, m % 2, s], w_hi[:, c, r], w_lo[:, c, r],
                                        m == 0, m == M - 1)
                ins.then_inc(h_used, 1)

            def group(g, scan, prep):
                for m in range(M):
                    ffn1(g, m)
                    if m == M - 1 and prep:
                        transpose_second(g + 1, 0)
                        transpose_second(g + 1, 1)
                    if m > 0:
                        ffn2(g, m - 1)
                    if scan and m == 10:
                        carry(NPAIR + g, t_bank[0][:])
                if prep:
                    transpose_second(g + 1, 2)
                    transpose_second(g + 1, 3)
                ffn2(g, M - 1)

            with pe.Fori(0, NB - NPAIR) as g:
                group(g, True, True)
            with pe.Fori(NB - NPAIR, NG - 1) as g:
                group(g, False, True)
            group(NG - 1, False, False)

        @block.vector
        def _(dve):
            own = Tally(dve_self)

            def step(ins):
                dve.wait_ge(dve_self, own.inc(ins))

            dve.memset(mask_i[:], 0).then_inc(mask_cleared, 1)
            step(dve.memset(one_row[:], 1.0))
            dve.sem_inc(h_split, ONE)

            def tile_stats(h, t):
                dve.wait_ge(xa_loaded[t], 16 * h + 16)
                wait_apart(dve, dve_self, own.inc(dve.bn_stats(st_a[:, t, :], xa[:, t, :])))
                dve.bn_aggr(mv_a[:, t, :], st_a[:, t, :]).then_inc(mv_a_ready, 1)

            def tile_norm(h, t):
                n = PT * h + t
                dve.wait_ge(ra_ready, n + 1)
                if not isinstance(n, int) or n >= 2:
                    dve.wait_ge(t_done, n - 1)
                dve.tensor_scalar(na[:, t % 2, :], xa[:, t, :], mv_a[:, t, 0:1], ra[:, t:t + 1],
                                  ALU.subtract, ALU.mult).then_inc(n_ready, 1)

            def tile_low(h, t):
                n = PT * h + t
                dve.wait_ge(t_hi, n + 1)
                dve.tensor_tensor(h_lo[:, t % 2, :], t_bank[t % 2][:], h_hi[:, t % 2, :].bitcast(F32),
                                  ALU.subtract).then_inc(t_lo, 1)

            def tile_add(h, t):
                n = PT * h + t
                dve.wait_ge(h_used, n + 1)
                if not isinstance(n, int) or n >= 2:
                    dve.wait_ge(xb_stored[t % 2], 16 * (PT // 2 * h + t // 2))
                dve.tensor_tensor(xb[:, t % 2, :], acc[t % TI][:], xa[:, t, :], ALU.add).then_inc(acc_read, 1)

            def scan_rows(b):
                dve.wait_ge(scaled, R * b + R)
                for j in range(1, R):
                    step(dve.scalar_tensor_tensor(cl[:, j, :], cl[:, j - 1, :], A, cl[:, j, :], ALU.mult, ALU.add))
                step(dve.tensor_copy(l3_hi[:], cl[:, R - 1, :]))
                dve.tensor_tensor(l3_lo[:], cl[:, R - 1, :], l3_hi[:].bitcast(F32), ALU.subtract).then_inc(l3_ready, 1)

            def add_carry(b, src):
                dve.wait_ge(carried, b + 1)
                dve.wait_ge(l3_ready, b + 1)
                for j in range(R):
                    ins = dve.scalar_tensor_tensor(cl[:, j, :], src, A ** (j + 1), cl[:, j, :], ALU.mult, ALU.add)
                ins.then_inc(block_ready, 1)

            def bits(out_, in_, a, op0, b=None, op1=None):
                if op1 is None:
                    step(dve.tensor_scalar(out_, in_, a, None, op0))
                else:
                    step(dve.tensor_scalar(out_, in_, a, b, op0, op1))

            LOW = 2047
            dve.wait_ge(mask_loaded, 32)
            bits(part_i[:, 0, :], mask_i[:], LOW, ALU.bitwise_and)
            bits(part_i[:, 1, :], mask_i[:], 11, ALU.logical_shift_right, LOW, ALU.bitwise_and)
            bits(part_i[:, 2, :], mask_i[:], 22, ALU.logical_shift_right, 1023, ALU.bitwise_and)
            step(dve.tensor_copy(part_f[:], part_i[:]))
            for v in range(3):
                step(dve.tensor_tensor_scan(cum_f[:, v, :], one_row[:], part_f[:, v, :], 0.0, ALU.mult, ALU.add))
            for v in range(3):
                ins = dve.tensor_copy(part_f[:, v, 0:1], cum_f[:, v, MJ - 1:MJ])
                step(ins)
            dve.sem_inc(tot_ready, 1)
            tile_stats(0, 0)
            dve.wait_ge(tot_summed, 1)
            step(dve.tensor_tensor(cum_f[:], cum_f[:], h_bank[1][:, 0:3].unsqueeze(2).to_broadcast([P, 3, MJ]), ALU.add))
            step(dve.tensor_copy(cum_i[:], cum_f[:]))
            bits(ia[:], cum_i[:, 0, :], 11, ALU.logical_shift_right)
            step(dve.tensor_tensor(ib[:], cum_f[:, 1, :], ia[:], ALU.add))
            bits(ia[:], ib[:], 11, ALU.logical_shift_right)
            step(dve.tensor_tensor(ic[:], cum_f[:, 2, :], ia[:], ALU.add))
            bits(cum_i[:, 2, :], ic[:], 22, ALU.logical_shift_left)
            bits(cum_i[:, 1, :], ib[:], LOW, ALU.bitwise_and, 11, ALU.logical_shift_left)
            bits(cum_i[:, 0, :], cum_i[:, 0, :], LOW, ALU.bitwise_and)
            step(dve.tensor_tensor(ia[:], cum_i[:, 0, :], cum_i[:, 1, :], ALU.bitwise_or))
            step(dve.tensor_tensor(ia[:], ia[:], cum_i[:, 2, :], ALU.bitwise_or))
            step(dve.tensor_copy(fa[:], ia[:]))
            step(dve.tensor_scalar(fa[:], fa[:], -1.0, None, ALU.add))
            step(dve.tensor_scalar(fb[:], fa[:], 0.0, float(S), ALU.is_lt, ALU.mult))
            step(dve.tensor_tensor(fa[:], fa[:], fb[:], ALU.add))
            step(dve.tensor_scalar(ia[:], fa[:], -1.0, float(S), ALU.max, ALU.min))
            bits(ib[:], ia[:], 2, ALU.arith_shift_right, P - 1, ALU.bitwise_and)
            step(dve.tensor_copy(pos_p[:], ib[:]))
            bits(ib[:], ia[:], 9, ALU.arith_shift_right, 2, ALU.logical_shift_left)
            bits(ic[:], ia[:], TI - 1, ALU.bitwise_and)
            step(dve.tensor_tensor(ib[:], ib[:], ic[:], ALU.bitwise_or))
            step(dve.tensor_copy(pos_q[:], ib[:]))
            dve.wait_ge(consts_made, 4)
            tile_norm(0, 0)
            step(dve.tensor_tensor(oh_p[:], pos_p[:].unsqueeze(2).to_broadcast([P, MJ, P]),
                                   iota_p[:].unsqueeze(1).to_broadcast([P, MJ, P]), ALU.is_equal))
            dve.tensor_tensor(oh_q[:], pos_q[:].unsqueeze(2).to_broadcast([P, MJ, NT]),
                              iota_p[:, 0:NT].unsqueeze(1).to_broadcast([P, MJ, NT]), ALU.is_equal).then_inc(onehots, 1)
            tile_stats(0, 1)
            dve.wait_ge(small_loaded, 16 * 5)
            for k in range(K):
                dve.wait_ge(win_hi_done, k + 1)
                dve.scalar_tensor_tensor(win_lo[:, k, :], acc[k][:], g_res_c[:, k:k + 1], win_hi[:, k, :].bitcast(F32),
                                         ALU.mult, ALU.subtract).then_inc(win_lo_done, 1)
            dve.wait_ge(consts_made, 5)
            step(dve.tensor_copy(band_hi[:], band[:]))
            dve.tensor_tensor(band_lo[:], band[:], band_hi[:].bitcast(F32), ALU.subtract).then_inc(band_ready, 1)
            dve.wait_ge(counted, 1)
            step(dve.tensor_scalar(cnt[:].rearrange("p g i -> p (g i)"), h_bank[0][:, 0:NT], 1.0, None, ALU.min))
            for i in range(1, TI):
                step(dve.tensor_tensor(cnt[:, :, i], cnt[:, :, i], cnt[:, :, i - 1], ALU.add))
            dve.tensor_copy(row_tot[:], cnt[:, :, TI - 1]).then_inc(cnt_ready, 1)
            dve.wait_ge(cnt_summed, 1)
            step(dve.tensor_copy(grp[:], h_bank[1][:, 64:64 + NG]))
            step(dve.tensor_tensor_scan(fa[:, 0:NG], one_row[:, 0:NG], grp[:], -1.0, ALU.mult, ALU.add))
            step(dve.tensor_tensor(fa[:, 0:NG], fa[:, 0:NG], grp[:], ALU.subtract))
            step(dve.tensor_tensor(fa[:, 0:NG], fa[:, 0:NG], h_bank[1][:, 0:NG], ALU.add))
            step(dve.tensor_tensor(plug_f[:], cnt[:], fa[:, 0:NG].unsqueeze(2).to_broadcast([P, NG, TI]), ALU.add))
            dve.tensor_scalar(plug[:], plug_f[:].rearrange("p g i -> p (g i)"), 0.0, None, ALU.max).then_inc(plug_ready, 1)

            def second_stats(g, i):
                dve.wait_ge(x1_ready, TI * g + i + 1)
                wait_apart(dve, dve_self, own.inc(dve.bn_stats(st_b[:, i, :], x_next[:, i, :])))
                dve.bn_aggr(mv_b[:, i, :], st_b[:, i, :]).then_inc(mv_b_ready, 1)

            def second_norm(g, i):
                dve.wait_ge(mv_b_ready, TI * (g + 1))
                dve.wait_ge(rb_ready, g + 1)
                if not isinstance(g, int) or g > 0:
                    dve.wait_ge(t_done, NT + TI * g)
                dve.tensor_scalar(n_rows[:, i, :], x_next[:, i, :], mv_b[:, i, 0:1], rb[:, i:i + 1],
                                  ALU.subtract, ALU.mult).then_inc(n_ready, 1)

            def transposed_low(g, i):
                dve.wait_ge(t_hi, NT + TI * g + i + 1)
                dve.tensor_tensor(xt_lo[:, :, i * P:(i + 1) * P], t_bank[i % 2][:].rearrange("p (k r) -> p k r", k=K),
                                  xt_hi[:, :, i * P:(i + 1) * P].bitcast(F32), ALU.subtract).then_inc(t_lo, 1)

            def pair(h, last=False):
                for t in range(PT):
                    n = PT * h + t
                    if not (isinstance(h, int) and n == 0):
                        tile_low(h, t)
                    if not last or t + 1 < PT:
                        tile_norm(h + (t + 1) // PT, (t + 1) % PT)
                    if not last or t + 2 < PT:
                        tile_stats(h + (t + 2) // PT, (t + 2) % PT)
                    if not (isinstance(h, int) and n == 0):
                        tile_add(h + (t - 1) // PT if t else h - 1, (t - 1) % PT)
                    if t == 6:
                        scan_rows(h)
                    if t == 7:
                        add_carry(h, h_bank[0][:])
                    if last and t >= PT - 2:
                        second_stats(0, 2 * (t - PT + 2))
                        second_stats(0, 2 * (t - PT + 2) + 1)

            tile_low(0, 0)
            pair(0)
            with dve.Fori(1, NPAIR - 1) as h:
                own.looped(h, 1, PT + R)
                pair(h)
            own.left(NPAIR - 2)
            pair(NPAIR - 1, last=True)
            for i in range(TI):
                second_norm(0, i)
            tile_add(NPAIR - 1, PT - 1)
            dve.wait_ge(h_used, NT)
            for i in range(TI):
                transposed_low(0, i)

            def group(g, scan, prep):
                for m in range(M):
                    dve.wait_ge(gelu_done, CREDIT + M * g + m + 1)
                    dve.wait_ge(h_used, NT + M * g + m - 1)
                    dve.tensor_tensor(h_lo[:, m % 2, :], g_f32[:], h_hi[:, m % 2, :].bitcast(F32),
                                      ALU.subtract).then_inc(h_split, 1)
                    if scan and m == 8:
                        scan_rows(NPAIR + g)
                    if scan and m == 11:
                        add_carry(NPAIR + g, t_bank[0][:])
                    if prep and m in (9, 10):
                        for i in (2 * (m - 9), 2 * (m - 9) + 1):
                            second_stats(g + 1, i)
                    if prep and m in (12, 13):
                        for i in (2 * (m - 12), 2 * (m - 12) + 1):
                            second_norm(g + 1, i)
                if prep:
                    for i in range(TI):
                        transposed_low(g + 1, i)
                dve.wait_ge(h_used, NT + M * (g + 1))
                dve.wait_ge(x_cur_ready, g + 1)
                for i in range(TI):
                    dve.tensor_tensor(x_cur[:, i, :], acc[i][:], x_cur[:, i, :], ALU.add).then_inc(acc_read, 1)

            with dve.Fori(0, NB - NPAIR) as g:
                own.looped(g, 0, R + TI)
                group(g, True, True)
            own.left(NB - NPAIR)
            with dve.Fori(NB - NPAIR, NG - 1) as g:
                own.looped(g, NB - NPAIR, TI)
                group(g, False, True)
            own.left(NG - 1 - (NB - NPAIR))
            group(NG - 1, False, False)


_INS = ['x', 'ctx_2048', 'mask_BxS2_if0', 'L0_xattn_W_in', 'L0_xattn_b_in', 'L0_xattn_g_res', 'L0_xattn_g_init',
        'L0_ffn_w1', 'L0_ffn_b1', 'L0_ffn_w2', 'L0_ffn_b2']
_OUTS = [((1, S, D), 'float32')]


def kernel(**inputs):
    import numpy as _np
    import concourse.bacc as _bacc
    from concourse import mybir as _mybir
    from concourse.bass_utils import run_bass_kernel_spmd as _run

    nc = _bacc.Bacc("TRN2", target_bir_lowering=False, num_devices=1)
    arrays, args = {}, []
    for name in _INS:
        a = _np.ascontiguousarray(inputs[name])
        arrays[f"in_{name}_dram"] = a
        args.append(nc.dram_tensor(f"in_{name}_dram", a.shape, _mybir.dt.from_np(a.dtype), kind="ExternalInput").ap())
    for i, (shape, dtype) in enumerate(_OUTS):
        dt = _mybir.dt.from_np(_np.dtype(dtype))
        args.append(nc.dram_tensor(f"out_{i}_dram", shape, dt, kind="ExternalOutput").ap())
    xattn_ffn(nc, *args)
    r = _run(nc, [arrays], core_ids=[0])
    return r.results[0]["out_0_dram"]
```

```python
import math
from contextlib import ExitStack

import concourse.bass as bass
from concourse import mybir

ALU = mybir.AluOpType
ACT = mybir.ActivationFunctionType
F32 = mybir.dt.float32
F32R = mybir.dt.float32r
BF16 = mybir.dt.bfloat16
I32 = mybir.dt.int32
U32 = mybir.dt.uint32

P = 128
S, D, HID = 4096, 512, 2048
CTX, DG = 3202, 1024
TI = 4
GR = P * TI
NG = S // GR
NT = S // P
K = D // P
M = HID // P
PT = 8
NPAIR = NT // PT
AHEAD = PT - 2
LEAD = 2
R = 4
BLK = P * R
HIST = 16
HP = HIST // R
NB = 7
STEP = BLK - HIST
START1 = CTX - BLK - STEP * (NB - 2)
FIRST_ROWS = START1 + HIST
MJ = 26
WCH = 8
WC = 2048

LN_EPS = 1e-5
RMS_EPS = 1e-5
A = -math.expm1(-0.001)
B_COEF = math.exp(-0.001)

CREDIT = 2
ONE = 1


def wait_apart(engine, sem, value):
    engine.wait_ge(sem, value)
    engine.nop(nofuse=True)


class Tally:

    def __init__(self, sem):
        self.sem, self.n, self.base = sem, 0, 0

    def inc(self, ins):
        ins.then_inc(self.sem, 1)
        self.n += 1
        return self.base + self.n

    def looped(self, i, first, per):
        self.entered, self.per = self.n, per
        self.base = (i - first) * per

    def left(self, turns):
        assert self.n - self.entered == self.per, (self.n - self.entered, self.per)
        self.base = 0
        self.n = self.entered + turns * self.per


def xattn_ffn(nc, x, ctx, mask, w_in, b_in, g_res, g_init, w1, b1, w2, b2, out):
    x_v = x.rearrange("b (g p i) d -> (b g) p i d", p=P, i=TI)
    out_v = out.rearrange("b (g p i) d -> (b g) p i d", p=P, i=TI)
    ctx_v = ctx.rearrange("b s d -> (b s) d")
    mask_v = mask.rearrange("b s -> (b s)")
    w1_v = w1.rearrange("(k p) n -> k p n", p=P)
    w2_v = w2.rearrange("(c m p) n -> c p m n", m=4, p=P)
    win_v = w_in.rearrange("(c p) d -> p c d", p=P)
    x1_dram = nc.dram_tensor("x1_part", [NG, P, TI, D], F32, kind="Internal").ap()
    table = nc.dram_tensor("scan_table", [CTX, D], F32, kind="Internal").ap()

    es = ExitStack()
    with es:
        def sb(name, shape, dt=F32):
            return es.enter_context(nc.sbuf_tensor(name, shape, dt))

        def sem(name):
            return es.enter_context(nc.semaphore(name))

        HEAD = 2 * WCH * WC * 4
        KB = 1024
        SLAB = HEAD + (16 + 8 + 8 + 8 + 4 + 2 + 4 + 4 + 8 + 4 + 2 + 2) * KB
        slab = sb("slab", [P, SLAB // 4])
        at = [nc.sbuf_base - SLAB]

        def place(name, shape, dt=F32, size=0, offset=None):
            where = at[0] if offset is None else offset
            t = nc.alloc_sbuf_tensor_at(name, shape, dt, offset=where)
            if offset is None:
                at[0] += size
            return t

        w_hi_at = at[0]
        w_hi = place("w_hi", [P, WCH, WC], F32R, WCH * WC * 4)
        w_lo_at = at[0]
        w_lo = place("w_lo", [P, WCH, WC], F32R, WCH * WC * 4)
        w_raw = place("w_raw", [P, WCH, WC], F32, offset=w_lo_at)
        xt_at = at[0]
        xt_hi = place("xt_hi", [P, K, GR], F32R, 8 * KB)
        xt_lo = place("xt_lo", [P, K, GR], F32R, 8 * KB)
        win_hi = place("win_hi", [P, K, D], F32R, offset=xt_at)
        win_lo = place("win_lo", [P, K, D], F32R, offset=xt_at + 8 * KB)
        x_cur_at = at[0]
        x_cur = place("x_cur", [P, TI, D], F32, 8 * KB)
        x_next_at = at[0]
        x_next = place("x_next", [P, TI, D], F32, 8 * KB)
        n_rows = place("n_rows", [P, TI, D], F32, 8 * KB)
        dep = place("dep", [P, 2, D], F32, 4 * KB)
        g_f32 = place("g_f32", [P, D], F32, 2 * KB)
        h_hi = place("h_hi", [P, 2, GR], F32R, 4 * KB)
        h_lo = place("h_lo", [P, 2, GR], F32R, 4 * KB)
        cl = place("cl", [P, R, D], F32, 8 * KB)
        ch = place("ch", [P, 2, D], F32, 4 * KB)
        l3_hi = place("l3_hi", [P, D], F32R, 2 * KB)
        l3_lo = place("l3_lo", [P, D], F32R, 2 * KB)
        xa = place("xa", [P, PT, D], F32, offset=w_hi_at + 6 * WC * 4)
        oh_p = place("oh_p", [P, MJ, P], BF16, offset=w_hi_at + 5 * WC * 4)
        win_raw = place("win_raw", [P, K, D], F32, offset=w_hi_at + 4 * WC * 4)
        early_at = [x_next_at]

        def early(name, shape, dt=F32):
            t = place(name, shape, dt, offset=early_at[0])
            n = 2 if dt == BF16 else 4
            for v in shape[1:]:
                n *= v
            early_at[0] += -(-n // 32) * 32
            assert early_at[0] <= x_next_at + 8 * KB
            return t

        oh_q = early("oh_q", [P, MJ, NT], BF16)
        cs = place("cs", [P, R, D], F32, offset=x_next_at)
        xb = place("xb", [P, 2, D], F32, offset=x_cur_at)
        na = place("na", [P, 2, D], F32, offset=x_cur_at + 4 * KB)

        b_in_b = sb("b_in_b", [P, D])
        b2_b = sb("b2_b", [P, D])
        g_init_b = sb("g_init_b", [P, D])
        ident = sb("ident", [P, P])
        tri = early("tri", [P, P])
        ones = early("ones", [P, P])
        band = early("band", [P, P])
        band_hi = sb("band_hi", [P, P], F32R)
        band_lo = sb("band_lo", [P, P], F32R)
        iota_p = early("iota_p", [P, P])
        b1_c = sb("b1_c", [P, M])
        g_res_c = sb("g_res_c", [P, K])
        neg_half = sb("neg_half", [P, TI])
        st_a = sb("st_a", [P, PT, 6])
        mv_a = sb("mv_a", [P, PT, 2])
        va_a = sb("va_a", [P, PT])
        ra = sb("ra", [P, PT])
        st_b = sb("st_b", [P, TI, 6])
        mv_b = sb("mv_b", [P, TI, 2])
        va_b = sb("va_b", [P, TI])
        rb = sb("rb", [P, TI])
        ss_h = sb("ss_h", [P, R])
        ss_l = sb("ss_l", [P, R])
        ss = sb("ss", [P, R])
        rc = sb("rc", [P, R])
        mask_i = early("mask_i", [P, MJ], I32)
        part_i = early("part_i", [P, 3, MJ], I32)
        part_f = early("part_f", [P, 3, MJ])
        cum_f = early("cum_f", [P, 3, MJ])
        one_row = early("one_row", [P, MJ])
        cum_i = early("cum_i", [P, 3, MJ], I32)
        ia = early("ia", [P, MJ], I32)
        ib = early("ib", [P, MJ], I32)
        ic = early("ic", [P, MJ], I32)
        fa = early("fa", [P, MJ])
        fb = early("fb", [P, MJ])
        pos_p = early("pos_p", [P, MJ])
        pos_q = early("pos_q", [P, MJ])
        cnt = early("cnt", [P, NG, TI])
        row_tot = early("row_tot", [P, NG])
        grp = early("grp", [P, NG])
        plug_f = early("plug_f", [P, NG, TI])
        plug = sb("plug", [P, NT], I32)
        idx = sb("idx", [P, TI], I32)

        def bank(name):
            return es.enter_context(nc.psum_tensor(name, [P, 512], F32))

        t_bank = [bank(f"t_bank{i}") for i in range(2)]
        h_bank = [bank(f"h_bank{i}") for i in range(2)]
        acc = [bank(f"acc{i}") for i in range(TI)]

        mask_loaded = sem("mask_loaded")
        win_loaded = sem("win_loaded")
        g_res_loaded = sem("g_res_loaded")
        small_loaded = sem("small_loaded")
        xa_loaded = [sem(f"xa_loaded{i}") for i in range(PT)]
        xb_stored = [sem(f"xb_stored{i}") for i in range(2)]
        w_loaded = [sem(f"w_loaded{i}") for i in range(WCH)]
        cl_loaded = sem("cl_loaded")
        ch_loaded = [sem(f"ch_loaded{i}") for i in range(2)]
        table_stored = sem("table_stored")
        x_next_loaded = sem("x_next_loaded")
        gathered = [sem(f"gathered{i}") for i in range(2)]
        out_stored = sem("out_stored")
        consts_made = sem("consts_made")
        mask_cleared = sem("mask_cleared")
        tot_ready = sem("tot_ready")
        tot_summed = sem("tot_summed")
        onehots = sem("onehots")
        counted = sem("counted")
        cnt_ready = sem("cnt_ready")
        cnt_summed = sem("cnt_summed")
        plug_ready = sem("plug_ready")
        band_ready = sem("band_ready")
        win_t = sem("win_t")
        win_hi_done = sem("win_hi_done")
        win_lo_done = sem("win_lo_done")
        mv_a_ready = sem("mv_a_ready")
        ra_ready = sem("ra_ready")
        n_ready = sem("n_ready")
        t_done = sem("t_done")
        t_hi = sem("t_hi")
        t_lo = sem("t_lo")
        acc_done = sem("acc_done")
        h_used = sem("h_used")
        acc_read = sem("acc_read")
        w_hi_done = sem("w_hi_done")
        w_lo_done = sem("w_lo_done")
        w_late = sem("w_late")
        sq_done = sem("sq_done")
        rc_ready = sem("rc_ready")
        scaled = sem("scaled")
        l3_ready = sem("l3_ready")
        carried = sem("carried")
        block_ready = sem("block_ready")
        idx_ready = sem("idx_ready")
        x1_ready = sem("x1_ready")
        mv_b_ready = sem("mv_b_ready")
        rb_ready = sem("rb_ready")
        x_cur_ready = sem("x_cur_ready")
        ffn1_done = sem("ffn1_done")
        gelu_done = sem("gelu_done")
        h_split = sem("h_split")
        act_self = sem("act_self")
        dve_self = sem("dve_self")
        pool_self = sem("pool_self")

        block = es.enter_context(nc.Block())

        def block_start(b):
            return START1 + STEP * (b - 1)

        @block.sync
        def _(sp):
            sp.dma_start(xa[:, 0, :], x_v[0, :, 0, :]).then_inc(xa_loaded[0], 16)
            sp.dma_start(win_raw[:], win_v).then_inc(win_loaded, 16)
            wait_apart(sp, mask_cleared, 1)
            full = CTX // MJ
            sp.dma_start(mask_i[0:full, :], mask_v[0:full * MJ].rearrange("(p j) -> p j", j=MJ)).then_inc(mask_loaded, 16)
            sp.dma_start(mask_i[full:full + 1, 0:CTX - full * MJ],
                         mask_v[full * MJ:CTX].rearrange("(p j) -> p j", p=1)).then_inc(mask_loaded, 16)
            for t in range(1, AHEAD):
                sp.dma_start(xa[:, t, :], x_v[t // TI, :, t % TI, :]).then_inc(xa_loaded[t], 16)

            def rows_of(b):
                first_row = 0 if isinstance(b, int) and b == 0 else block_start(b)
                return ctx_v[bass.ds(first_row, BLK), :].rearrange("(p j) d -> p j d", j=R)

            def load_low_half(b):
                sp.dma_start(cl[:], rows_of(b)[:, :, 0:D]).then_inc(cl_loaded, 16)

            def load_high_half(b, j):
                if not isinstance(b, int) or R * b + j >= 2:
                    wait_apart(sp, sq_done, R * b + j - 1)
                sp.dma_start(ch[:, j % 2, :], rows_of(b)[:, j, D:DG]).then_inc(ch_loaded[j % 2], 16)

            def store_block(b, src):
                wait_apart(sp, block_ready, b + 1)
                if isinstance(b, int) and b == 0:
                    whole = FIRST_ROWS // R
                    sp.dma_start(table[0:whole * R, :].rearrange("(p j) d -> p j d", j=R),
                                 src[0:whole, :, :]).then_inc(table_stored, 16)
                    sp.dma_start(table[whole * R:FIRST_ROWS, :].rearrange("(p j) d -> p j d", p=1),
                                 src[whole:whole + 1, 0:FIRST_ROWS - whole * R, :]).then_inc(table_stored, 16)
                else:
                    sp.dma_start(table[bass.ds(block_start(b) + HIST, STEP), :].rearrange("(p j) d -> p j d", j=R),
                                 src[HP:P, :, :]).then_inc(table_stored, 16)

            def tile(h, t, more=True):
                h, t = h + t // PT, t % PT
                if not isinstance(h, int) or PT * h + t > 0:
                    wait_apart(sp, acc_read, PT * h + t)
                    v = (t - 1) % PT
                    g = 2 * h + (t - 1) // TI
                    sp.dma_start(x1_dram[g, :, v % TI, :], xb[:, v % 2, :]).then_inc(xb_stored[v % 2], 16)
                if more:
                    u = (t + AHEAD) % PT
                    g = 2 * h + (t + AHEAD) // TI
                    sp.dma_start(xa[:, u, :], x_v[g, :, u % TI, :]).then_inc(xa_loaded[u], 16)

            def span(h, last=False):
                for s in range(PT - LEAD if last else PT):
                    tile(h, LEAD + s, more=not last)
                    if s == 0:
                        if not isinstance(h, int) or h > 0:
                            wait_apart(sp, block_ready, h)
                        load_low_half(h)
                    if s == 3:
                        load_high_half(h, 2)
                    if s == 4:
                        load_high_half(h, 3)
                    if s == 5 and not last:
                        load_high_half(h + 1, 0)
                        load_high_half(h + 1, 1)
                    if s == 7:
                        store_block(h, cs)
                    if last and s == 2:
                        wait_apart(sp, table_stored, 16 * NPAIR)
                        wait_apart(sp, xb_stored[0], 16 * 2)
                        wait_apart(sp, xb_stored[1], 16 * 2)
                        wait_apart(sp, plug_ready, 1)
                        wait_apart(sp, band_ready, 1)
                        sp.dma_start(x_next[:], x1_dram[0, :, :, :]).then_inc(x_next_loaded, 16)

            load_high_half(0, 0)
            load_high_half(0, 1)
            for t in range(LEAD):
                tile(0, t)
            span(0)
            with sp.Fori(1, NPAIR - 1) as h:
                span(h)
            span(NPAIR - 1, last=True)
            wait_apart(sp, acc_read, NT)
            sp.dma_start(x1_dram[NG - 1, :, TI - 1, :], xb[:, 1, :]).then_inc(xb_stored[1], 16)
            store_block(NPAIR - 1, cl)
            for s in xb_stored:
                wait_apart(sp, s, 16 * NT // 2)

            def group(g, scan, prep):
                if scan:
                    b = NPAIR + g
                    wait_apart(sp, table_stored, 16 * b + 16)
                    load_high_half(b, 0)
                    load_high_half(b, 1)
                    load_low_half(b)
                if prep:
                    wait_apart(sp, x_cur_ready, g + 1)
                    sp.dma_start(x_next[:], x1_dram[g + 1, :, :, :]).then_inc(x_next_loaded, 16)
                if scan:
                    load_high_half(b, 2)
                    load_high_half(b, 3)
                    store_block(b, cl)
                for i in range(TI):
                    wait_apart(sp, acc_read, NT + TI * g + i + 1)
                    sp.dma_start(out_v[g, :, i, :], x_cur[:, i, :]).then_inc(out_stored, 16)

            with sp.Fori(0, NB - NPAIR) as g:
                group(g, True, True)
            with sp.Fori(NB - NPAIR, NG - 1) as g:
                group(g, False, True)
            group(NG - 1, False, False)
            wait_apart(sp, out_stored, 16 * TI * NG)
            wait_apart(sp, table_stored, 16 * (NB + 1))

        @block.gpsimd
        def _(pool):
            own = Tally(pool_self)

            def step(ins):
                wait_apart(pool, pool_self, own.inc(ins))

            pool.memset(ident[:], 0.0).then_inc(pool_self, 1)
            pool.memset(tri[:], 1.0).then_inc(pool_self, 1)
            pool.memset(band[:], 0.0).then_inc(pool_self, 1)
            own.n = 3
            pool.wait_ge(pool_self, 3)
            pool.affine_select(out=ident[:], in_=ident[:], compare_op=ALU.not_equal, fill=1.0, base=0,
                               pattern=[[-1, P]], channel_multiplier=1).then_inc(consts_made, 1)
            pool.affine_select(out=tri[:], in_=tri[:], compare_op=ALU.is_gt, fill=0.0, base=0,
                               pattern=[[1, P]], channel_multiplier=-1).then_inc(consts_made, 1)
            pool.memset(ones[:], 1.0).then_inc(consts_made, 1)
            pool.iota(iota_p[:], [[1, P]], base=0, channel_multiplier=0,
                      allow_small_or_imprecise_dtypes=True).then_inc(consts_made, 1)
            pool.memset(neg_half[:], -0.5).then_inc(pool_self, 1)
            own.n += 1
            for q in range(HP):
                step(pool.affine_select(out=band[:], in_=band[:], compare_op=ALU.not_equal, fill=A ** (R * q),
                                        base=q + 1, pattern=[[-1, P]], channel_multiplier=1))
            pool.sem_inc(consts_made, 1)

            def tile_scale(n, t):
                wait_apart(pool, mv_a_ready, n + 1)
                step(pool.tensor_scalar(va_a[:, t:t + 1], mv_a[:, t, 1:2], 1.0 + RMS_EPS, LN_EPS * RMS_EPS,
                                        ALU.mult, ALU.add))
                pool.tensor_tensor(ra[:, t:t + 1], va_a[:, t:t + 1], neg_half[:, 0:1], ALU.pow).then_inc(ra_ready, 1)

            def low_weights(c, q):
                pool.wait_ge(w_hi_done, c + 1)
                r = slice(q * D, (q + 1) * D)
                pool.tensor_tensor(w_lo[:, c, r], w_raw[:, c, r], w_hi[:, c, r].bitcast(F32),
                                   ALU.subtract).then_inc(w_lo_done, 1)

            def context_scale(b):
                pool.wait_ge(sq_done, R * b + R)
                step(pool.tensor_tensor(ss[:], ss_h[:], ss_l[:], ALU.add))
                step(pool.tensor_scalar(ss[:], ss[:], 1.0 / DG, RMS_EPS, ALU.mult, ALU.add))
                step(pool.tensor_tensor(rc[:], ss[:], neg_half[:], ALU.pow))
                pool.tensor_scalar(rc[:], rc[:], B_COEF, 1.0, ALU.mult, ALU.mult).then_inc(rc_ready, 1)

            def gather_indices(g):
                step(pool.tensor_copy(idx[:], plug[:, bass.ds(TI * g, TI)]))

            def gather(g, i, blocks):
                wait_apart(pool, table_stored, 16 * (blocks + 1))
                rows = table[0:block_start(blocks - 1) + BLK, :]
                pool.indirect_dma_start(dep[:, i % 2, :], None, rows, bass.IndirectOffsetOnAxis(
                    ap=idx[:, i:i + 1].bitcast(U32), axis=0)).then_inc(gathered[i % 2], 16)

            def add_context(g, i):
                pool.wait_ge(gathered[i % 2], 16 * (2 * g + i // 2 + 1))
                step(pool.tensor_tensor(dep[:, i % 2, :], dep[:, i % 2, :], g_init_b[:], ALU.mult))
                step(pool.tensor_tensor(dep[:, i % 2, :], dep[:, i % 2, :], b_in_b[:], ALU.add))
                ins = pool.tensor_tensor(x_next[:, i, :], x_next[:, i, :], dep[:, i % 2, :], ALU.add)
                ins.then_inc(x1_ready, 1)
                wait_apart(pool, x1_ready, TI * g + i + 1)

            def group_scale(g):
                wait_apart(pool, mv_b_ready, TI * (g + 1))
                step(pool.tensor_scalar(va_b[:], mv_b[:, :, 1], LN_EPS, 1.0, ALU.add, ALU.mult))
                pool.tensor_tensor(rb[:], va_b[:], neg_half[:], ALU.pow).then_inc(rb_ready, 1)

            def prepare(g, blocks):
                gather_indices(g)
                for i in range(2):
                    gather(g, i, blocks)
                pool.wait_ge(x_next_loaded, 16 * (g + 1))
                for i in range(TI):
                    add_context(g, i)
                    if i < 2:
                        gather(g, i + 2, blocks)

            def span(h, last=False):
                for s in range(PT - LEAD if last else PT):
                    t = LEAD + s
                    if not last or t + 2 < PT:
                        tile_scale(PT * h + t + 2, (t + 2) % PT)
                    if not last:
                        pieces = {4: (0, 1), 5: (2, 3), 7: (4, 5, 6, 7)}.get(s, ()) if isinstance(h, int) else (s,)
                        for v in pieces:
                            low_weights(2 * h + v // 4, v % 4)
                    if s == 4:
                        context_scale(h)
                    if last and s == 0:
                        pool.wait_ge(small_loaded, 16 * 4)
                        pool.wait_ge(plug_ready, 1)
                        gather_indices(0)
                        for i in (0, 1):
                            gather(0, i, 2)
                    if last and s in (3, 4):
                        if s == 3:
                            pool.wait_ge(x_next_loaded, 16)
                        for i in (2 * (s - 3), 2 * (s - 3) + 1):
                            add_context(0, i)
                            if s == 3:
                                gather(0, i + 2, 2)
                if last:
                    group_scale(0)

            tile_scale(0, 0)
            tile_scale(1, 1)
            tile_scale(2, 2)
            tile_scale(3, 3)
            span(0)
            with pool.Fori(1, NPAIR - 1) as h:
                own.looped(h, 1, PT + 3)
                span(h)
            own.left(NPAIR - 2)
            span(NPAIR - 1, last=True)
            pool.wait_ge(acc_read, NT)
            for c in (6, 7):
                pool.wait_ge(w_loaded[c], 16)
                step(pool.tensor_copy(w_hi[:, c, :], w_raw[:, c, :]))
                pool.tensor_tensor(w_lo[:, c, :], w_raw[:, c, :], w_hi[:, c, :].bitcast(F32),
                                   ALU.subtract).then_inc(w_late, 1)

            for s in xb_stored:
                pool.wait_ge(s, 16 * NT // 2)

            def group(g, scan, prep):
                pool.wait_ge(n_ready, NT + TI * (g + 1))
                if not isinstance(g, int) or g > 0:
                    pool.wait_ge(out_stored, 16 * TI * g)
                pool.tensor_tensor(x_cur[:], x_next[:], b2_b[:].unsqueeze(1).to_broadcast([P, TI, D]),
                                   ALU.add).then_inc(x_cur_ready, 1)
                if scan:
                    context_scale(NPAIR + g)
                if prep:
                    prepare(g + 1, g + 3 if scan else NB)
                    group_scale(g + 1)

            for g in range(NB - NPAIR):
                group(g, True, True)
            with pool.Fori(NB - NPAIR, NG - 1) as g:
                own.looped(g, NB - NPAIR, 1 + 2 * TI + 1)
                group(g, False, True)
            own.left(NG - 1 - (NB - NPAIR))
            group(NG - 1, False, False)

        @block.scalar
        def _(act):
            own = Tally(act_self)
            act.dma_start(g_res_c[:], g_res.rearrange("(k p) -> p k", p=P),
                          allow_slow_non_contiguous=True).then_inc(g_res_loaded, 16)

            def load_weights(c):
                v = w_raw[:, c, :]
                if c < 4:
                    act.dma_start(v, w1_v[c, :, :]).then_inc(w_loaded[c], 16)
                else:
                    act.dma_start(v.rearrange("p (m n) -> p m n", m=4), w2_v[c - 4, :, :, :]).then_inc(w_loaded[c], 16)

            act.wait_ge(consts_made, 1)
            act.activation(g_f32[:, 0:1], ident[:, 0:1], ACT.Gelu).then_inc(act_self, 1)
            own.n += 1
            act.wait_ge(g_res_loaded, 16)
            for k in range(K):
                act.wait_ge(win_t, k + 1)
                act.activation(win_hi[:, k, :], acc[k][:], ACT.Copy, scale=g_res_c[:, k:k + 1]).then_inc(win_hi_done, 1)

            def tile_high(n, t):
                act.wait_ge(t_done, n + 1)
                if not isinstance(n, int) or n >= 2:
                    act.wait_ge(h_used, n - 1)
                act.activation(h_hi[:, t % 2, :], t_bank[t % 2][:], ACT.Copy).then_inc(t_hi, 1)

            def squares(b, j):
                act.wait_ge(ch_loaded[j % 2], 16 * (2 * b + j // 2 + 1))
                v = own.inc(act.activation(ch[:, j % 2, :], ch[:, j % 2, :], ACT.Square, accum_out=ss_h[:, j:j + 1]))
                act.wait_ge(act_self, v)
                if j == 0:
                    act.wait_ge(cl_loaded, 16 * (b + 1))
                act.activation(ch[:, j % 2, :], cl[:, j, :], ACT.Square, accum_out=ss_l[:, j:j + 1]).then_inc(sq_done, 1)

            def scale_rows(b):
                act.wait_ge(rc_ready, b + 1)
                for j in range(R):
                    act.activation(cl[:, j, :], cl[:, j, :], ACT.Copy, scale=rc[:, j:j + 1]).then_inc(scaled, 1)

            def first_loads(n):
                load_weights(n)
                if n == 1:
                    act.dma_start(b1_c[:], b1.rearrange("(m p) -> p m", p=P),
                                  allow_slow_non_contiguous=True).then_inc(small_loaded, 16)
                    for v, src in ((b_in_b, b_in), (b2_b, b2), (g_init_b, g_init[0:D])):
                        act.dma_start(v[:], src.rearrange("(a n) -> a n", a=1).to_broadcast([P, D]))\
                           .then_inc(small_loaded, 16)

            def span(h, last=False):
                for s in range(PT - LEAD if last else PT):
                    t = LEAD + s
                    tile_high(PT * h + t, t % PT)
                    if isinstance(h, int) and h == 0 and t < WCH:
                        first_loads(t)
                    if s in ((3, 6) if isinstance(h, int) else (0, 1)) and not last:
                        c = 2 * h + (1 if s in (1, 6) else 0)
                        if isinstance(h, int):
                            act.wait_ge(w_loaded[c], 16)
                        act.activation(w_hi[:, c, :], w_raw[:, c, :], ACT.Copy).then_inc(w_hi_done, 1)
                    if s in (2, 3):
                        squares(h, s - 2)
                    if s == 4:
                        squares(h, 2)
                        squares(h, 3)
                    if s == 5:
                        scale_rows(h)

            for t in range(LEAD):
                tile_high(t, t)
                first_loads(t)
            span(0)
            act.wait_ge(counted, 1)
            for c in range(2, 6):
                act.wait_ge(w_loaded[c], 16)
            with act.Fori(1, NPAIR - 1) as h:
                own.looped(h, 1, R)
                span(h)
            own.left(NPAIR - 2)
            span(NPAIR - 1, last=True)
            act.sem_inc(gelu_done, CREDIT)
            act.wait_ge(small_loaded, 16 * 4)

            def transposed_high(g, i):
                act.wait_ge(t_done, NT + TI * g + i + 1)
                act.activation(xt_hi[:, :, i * P:(i + 1) * P], t_bank[i % 2][:].rearrange("p (k r) -> p k r", k=K),
                               ACT.Copy).then_inc(t_hi, 1)

            act.wait_ge(h_used, NT)
            for i in range(TI):
                transposed_high(0, i)

            def group(g, scan, prep):
                for m in range(M):
                    act.wait_ge(ffn1_done, M * g + m + 1)
                    act.wait_ge(h_used, NT + M * g + m - 1)
                    act.activation(h_hi[:, m % 2, :], h_bank[m % 2][:], ACT.Gelu, bias=b1_c[:, m:m + 1])
                    act.wait_ge(h_split, ONE + M * g + m)
                    act.activation(g_f32[:], h_bank[m % 2][:], ACT.Gelu, bias=b1_c[:, m:m + 1]).then_inc(gelu_done, 1)
                    if scan and 3 <= m < 3 + R:
                        squares(NPAIR + g, m - 3)
                    if scan and m == 8:
                        scale_rows(NPAIR + g)
                if prep:
                    for i in range(TI):
                        transposed_high(g + 1, i)

            with act.Fori(0, NB - NPAIR) as g:
                own.looped(g, 0, R)
                group(g, True, True)
            own.left(NB - NPAIR)
            with act.Fori(NB - NPAIR, NG - 1) as g:
                group(g, False, True)
            group(NG - 1, False, False)

        @block.tensor
        def _(pe):
            pe.wait_ge(consts_made, 4)
            pe.wait_ge(win_loaded, 16)
            for k in range(K):
                for c in range(K):
                    ins = nc.tensor.transpose(acc[k][:, c * P:(c + 1) * P], win_raw[:, c, k * P:(k + 1) * P], ident[:])
                ins.then_inc(win_t, 1)

            def transpose_first(n, t):
                pe.wait_ge(n_ready, n + 1)
                if not isinstance(n, int) or n >= 2:
                    pe.wait_ge(t_lo, n - 1)
                for k in range(K):
                    ins = nc.tensor.transpose(t_bank[t % 2][:, k * P:(k + 1) * P], na[:, t % 2, k * P:(k + 1) * P], ident[:])
                ins.then_inc(t_done, 1)

            def split_product(dst, a_hi, a_lo, b_hi, b_lo, first, final):
                nc.tensor.matmul(dst, a_hi, b_hi, start=first, stop=False)
                nc.tensor.matmul(dst, a_hi, b_lo, start=False, stop=False)
                return nc.tensor.matmul(dst, a_lo, b_hi, start=False, stop=final)

            def project(n, t):
                first = isinstance(n, int) and n == 0
                pe.wait_ge(t_lo, n + 1)
                if not isinstance(n, int) or n >= TI:
                    pe.wait_ge(acc_read, n - TI + 1)
                for k in range(K):
                    c = slice(k * P, (k + 1) * P)
                    if first:
                        pe.wait_ge(win_hi_done, k + 1)
                        pe.wait_ge(win_lo_done, k + 1)
                    ins = split_product(acc[t % TI][:], h_hi[:, t % 2, c], h_lo[:, t % 2, c],
                                        win_hi[:, k, :], win_lo[:, k, :], k == 0, k == K - 1)
                ins.then_inc(h_used, 1)

            def carry(b, dst):
                pe.wait_ge(l3_ready, b + 1)
                split_product(dst, band_hi[:], band_lo[:], l3_hi[:], l3_lo[:], True, True).then_inc(carried, 1)

            def mask_totals():
                pe.wait_ge(tot_ready, 1)
                nc.tensor.matmul(h_bank[1][:, 0:3], tri[:], part_f[:, :, 0], start=True, stop=True).then_inc(tot_summed, 1)

            def count_positions():
                pe.wait_ge(onehots, 1)
                for j in range(MJ):
                    ins = nc.tensor.matmul(h_bank[0][:, 0:NT], oh_p[:, j, :], oh_q[:, j, :], start=(j == 0), stop=(j == MJ - 1))
                ins.then_inc(counted, 1)

            def count_before():
                pe.wait_ge(cnt_ready, 1)
                nc.tensor.matmul(h_bank[1][:, 0:NG], tri[:], row_tot[:], start=True, stop=True)
                nc.tensor.matmul(h_bank[1][:, 64:64 + NG], ones[:], row_tot[:], start=True, stop=True).then_inc(cnt_summed, 1)

            def transpose_second(g, i):
                pe.wait_ge(n_ready, NT + TI * g + i + 1)
                pe.wait_ge(t_lo, NT + TI * g + i - 1)
                for k in range(K):
                    ins = nc.tensor.transpose(t_bank[i % 2][:, k * P:(k + 1) * P], n_rows[:, i, k * P:(k + 1) * P], ident[:])
                ins.then_inc(t_done, 1)

            def tile(n, t, more=True):
                if more:
                    transpose_first(n + 1, (t + 1) % PT)
                project(n, t)

            def span(h, last=False):
                for s in range(PT - LEAD if last else PT):
                    t = LEAD + s
                    tile(PT * h + t, t % PT, more=not (last and t + 1 == PT))
                    if isinstance(h, int) and h == 0:
                        if s == 3:
                            count_positions()
                        if s == 5:
                            count_before()
                            pe.wait_ge(band_ready, 1)
                    if s == 6:
                        carry(h, h_bank[0][:])

            transpose_first(0, 0)
            mask_totals()
            for t in range(LEAD):
                tile(t, t)
            span(0)
            with pe.Fori(1, NPAIR - 1) as h:
                span(h)
            span(NPAIR - 1, last=True)
            pe.wait_ge(acc_read, NT - 2)
            carry(NPAIR - 1, acc[1][:])
            for i in range(TI):
                transpose_second(0, i)

            pe.wait_ge(w_lo_done, 6 * 4)
            pe.wait_ge(w_hi_done, 6)

            def ffn1(g, m):
                pe.wait_ge(gelu_done, M * g + m + 1)
                if m == 0:
                    pe.wait_ge(t_hi, NT + TI * (g + 1))
                    pe.wait_ge(t_lo, NT + TI * (g + 1))
                for k in range(K):
                    c = slice(m * P, (m + 1) * P)
                    ins = split_product(h_bank[m % 2][:], w_hi[:, k, c], w_lo[:, k, c], xt_hi[:, k, :], xt_lo[:, k, :],
                                        k == 0, k == K - 1)
                ins.then_inc(ffn1_done, 1)

            def ffn2(g, m):
                pe.wait_ge(h_split, ONE + M * g + m + 1)
                if m == 0:
                    pe.wait_ge(acc_read, NT + TI * g)
                if m == 8:
                    pe.wait_ge(w_late, 2)
                c, r = 4 + m // 4, slice((m % 4) * D, (m % 4 + 1) * D)
                for i in range(TI):
                    s = slice(i * P, (i + 1) * P)
                    ins = split_product(acc[i][:], h_hi[:, m % 2, s], h_lo[:, m % 2, s], w_hi[:, c, r], w_lo[:, c, r],
                                        m == 0, m == M - 1)
                    if m == M - 1 and i < TI - 1:
                        ins.then_inc(acc_done, 1)
                ins.then_inc(h_used, 1)

            def group(g, scan, prep):
                for m in range(M):
                    ffn1(g, m)
                    if m == M - 1 and prep:
                        transpose_second(g + 1, 0)
                        transpose_second(g + 1, 1)
                    if m > 0:
                        ffn2(g, m - 1)
                    if scan and m == 11:
                        carry(NPAIR + g, t_bank[0][:])
                if prep:
                    transpose_second(g + 1, 2)
                    transpose_second(g + 1, 3)
                ffn2(g, M - 1)

            with pe.Fori(0, NB - NPAIR) as g:
                group(g, True, True)
            with pe.Fori(NB - NPAIR, NG - 1) as g:
                group(g, False, True)
            group(NG - 1, False, False)

        @block.vector
        def _(dve):
            own = Tally(dve_self)

            def step(ins):
                dve.wait_ge(dve_self, own.inc(ins))

            dve.memset(mask_i[:], 0).then_inc(mask_cleared, 1)
            step(dve.memset(one_row[:], 1.0))
            dve.sem_inc(h_split, ONE)

            def tile_stats(h, t):
                dve.wait_ge(xa_loaded[t], 16 * h + 16)
                wait_apart(dve, dve_self, own.inc(dve.bn_stats(st_a[:, t, :], xa[:, t, :])))
                dve.bn_aggr(mv_a[:, t, :], st_a[:, t, :]).then_inc(mv_a_ready, 1)

            def tile_norm(h, t):
                n = PT * h + t
                dve.wait_ge(ra_ready, n + 1)
                if not isinstance(n, int) or n >= 2:
                    dve.wait_ge(t_done, n - 1)
                dve.tensor_scalar(na[:, t % 2, :], xa[:, t, :], mv_a[:, t, 0:1], ra[:, t:t + 1],
                                  ALU.subtract, ALU.mult).then_inc(n_ready, 1)

            def tile_low(h, t):
                n = PT * h + t
                dve.wait_ge(t_hi, n + 1)
                dve.tensor_tensor(h_lo[:, t % 2, :], t_bank[t % 2][:], h_hi[:, t % 2, :].bitcast(F32),
                                  ALU.subtract).then_inc(t_lo, 1)

            def tile_add(h, t):
                n = PT * h + t
                dve.wait_ge(h_used, n + 1)
                if not isinstance(n, int) or n >= 2:
                    dve.wait_ge(xb_stored[t % 2], 16 * (PT // 2 * h + t // 2))
                dve.tensor_tensor(xb[:, t % 2, :], acc[t % TI][:], xa[:, t, :], ALU.add).then_inc(acc_read, 1)

            def scan_rows(b):
                dve.wait_ge(scaled, R * b + R)
                for j in range(1, R):
                    step(dve.scalar_tensor_tensor(cl[:, j, :], cl[:, j - 1, :], A, cl[:, j, :], ALU.mult, ALU.add))
                step(dve.tensor_copy(l3_hi[:], cl[:, R - 1, :]))
                dve.tensor_tensor(l3_lo[:], cl[:, R - 1, :], l3_hi[:].bitcast(F32), ALU.subtract).then_inc(l3_ready, 1)

            def add_carry(b, src, dst):
                dve.wait_ge(carried, b + 1)
                if not isinstance(b, int):
                    dve.wait_ge(table_stored, 16 * b + 16)
                for j in range(R):
                    ins = dve.scalar_tensor_tensor(dst[:, j, :], src, A ** (j + 1), cl[:, j, :], ALU.mult, ALU.add)
                ins.then_inc(block_ready, 1)

            def bits(out_, in_, a, op0, b=None, op1=None):
                if op1 is None:
                    step(dve.tensor_scalar(out_, in_, a, None, op0))
                else:
                    step(dve.tensor_scalar(out_, in_, a, b, op0, op1))

            def mask_parts():
                dve.wait_ge(mask_loaded, 32)
                bits(part_i[:, 0, :], mask_i[:], LOW, ALU.bitwise_and)
                bits(part_i[:, 1, :], mask_i[:], 11, ALU.logical_shift_right, LOW, ALU.bitwise_and)
                bits(part_i[:, 2, :], mask_i[:], 22, ALU.logical_shift_right, 1023, ALU.bitwise_and)
                step(dve.tensor_copy(part_f[:], part_i[:]))
                for v in range(3):
                    step(dve.tensor_tensor_scan(cum_f[:, v, :], one_row[:], part_f[:, v, :], 0.0, ALU.mult, ALU.add))
                dve.tensor_copy(part_f[:, :, 0], cum_f[:, :, MJ - 1]).then_inc(tot_ready, 1)

            def mask_positions():
                dve.wait_ge(tot_summed, 1)
                step(dve.tensor_tensor(cum_f[:], cum_f[:], h_bank[1][:, 0:3].unsqueeze(2).to_broadcast([P, 3, MJ]), ALU.add))
                step(dve.tensor_copy(cum_i[:], cum_f[:]))
                bits(ia[:], cum_i[:, 0, :], 11, ALU.logical_shift_right)
                step(dve.tensor_tensor(ib[:], cum_f[:, 1, :], ia[:], ALU.add))
                bits(ia[:], ib[:], 11, ALU.logical_shift_right)
                step(dve.tensor_tensor(ic[:], cum_f[:, 2, :], ia[:], ALU.add))
                bits(cum_i[:, 2, :], ic[:], 22, ALU.logical_shift_left)
                bits(cum_i[:, 1, :], ib[:], LOW, ALU.bitwise_and, 11, ALU.logical_shift_left)
                bits(cum_i[:, 0, :], cum_i[:, 0, :], LOW, ALU.bitwise_and)
                step(dve.tensor_tensor(ia[:], cum_i[:, 0, :], cum_i[:, 1, :], ALU.bitwise_or))
                step(dve.tensor_tensor(ia[:], ia[:], cum_i[:, 2, :], ALU.bitwise_or))

            def mask_places():
                step(dve.tensor_copy(fa[:], ia[:]))
                step(dve.tensor_scalar(fa[:], fa[:], -1.0, None, ALU.add))
                step(dve.tensor_scalar(fb[:], fa[:], 0.0, float(S), ALU.is_lt, ALU.mult))
                step(dve.tensor_tensor(fa[:], fa[:], fb[:], ALU.add))
                step(dve.tensor_scalar(ia[:], fa[:], -1.0, float(S), ALU.max, ALU.min))
                bits(ib[:], ia[:], 2, ALU.arith_shift_right, P - 1, ALU.bitwise_and)
                step(dve.tensor_copy(pos_p[:], ib[:]))
                bits(ib[:], ia[:], 9, ALU.arith_shift_right, 2, ALU.logical_shift_left)
                bits(ic[:], ia[:], TI - 1, ALU.bitwise_and)
                step(dve.tensor_tensor(ib[:], ib[:], ic[:], ALU.bitwise_or))
                step(dve.tensor_copy(pos_q[:], ib[:]))

            def one_hots_p(j0, j1):
                n = j1 - j0
                step(dve.tensor_tensor(oh_p[:, j0:j1, :], pos_p[:, j0:j1].unsqueeze(2).to_broadcast([P, n, P]),
                                       iota_p[:].unsqueeze(1).to_broadcast([P, n, P]), ALU.is_equal))

            def one_hots_q():
                dve.tensor_tensor(oh_q[:], pos_q[:].unsqueeze(2).to_broadcast([P, MJ, NT]),
                                  iota_p[:, 0:NT].unsqueeze(1).to_broadcast([P, MJ, NT]), ALU.is_equal).then_inc(onehots, 1)

            def low_w_in():
                dve.wait_ge(g_res_loaded, 16)
                for k in range(K):
                    dve.wait_ge(win_hi_done, k + 1)
                    dve.scalar_tensor_tensor(win_lo[:, k, :], acc[k][:], g_res_c[:, k:k + 1], win_hi[:, k, :].bitcast(F32),
                                             ALU.mult, ALU.subtract).then_inc(win_lo_done, 1)

            def split_band():
                dve.wait_ge(consts_made, 5)
                step(dve.tensor_copy(band_hi[:], band[:]))
                dve.tensor_tensor(band_lo[:], band[:], band_hi[:].bitcast(F32), ALU.subtract).then_inc(band_ready, 1)

            def count_rows():
                dve.wait_ge(counted, 1)
                step(dve.tensor_scalar(cnt[:].rearrange("p g i -> p (g i)"), h_bank[0][:, 0:NT], 1.0, None, ALU.min))
                for i in range(1, TI):
                    step(dve.tensor_tensor(cnt[:, :, i], cnt[:, :, i], cnt[:, :, i - 1], ALU.add))
                dve.tensor_copy(row_tot[:], cnt[:, :, TI - 1]).then_inc(cnt_ready, 1)

            def finish_plug():
                dve.wait_ge(cnt_summed, 1)
                step(dve.tensor_copy(grp[:], h_bank[1][:, 64:64 + NG]))
                step(dve.tensor_tensor_scan(fa[:, 0:NG], one_row[:, 0:NG], grp[:], -1.0, ALU.mult, ALU.add))
                step(dve.tensor_tensor(fa[:, 0:NG], fa[:, 0:NG], grp[:], ALU.subtract))
                step(dve.tensor_tensor(fa[:, 0:NG], fa[:, 0:NG], h_bank[1][:, 0:NG], ALU.add))
                step(dve.tensor_tensor(plug_f[:], cnt[:], fa[:, 0:NG].unsqueeze(2).to_broadcast([P, NG, TI]), ALU.add))
                dve.tensor_scalar(plug[:], plug_f[:].rearrange("p g i -> p (g i)"), 0.0, None, ALU.max).then_inc(plug_ready, 1)

            LOW = 2047
            tile_stats(0, 0)
            tile_stats(0, 1)
            tile_norm(0, 0)
            mask_parts()
            low_w_in()

            def second_stats(g, i):
                dve.wait_ge(x1_ready, TI * g + i + 1)
                wait_apart(dve, dve_self, own.inc(dve.bn_stats(st_b[:, i, :], x_next[:, i, :])))
                dve.bn_aggr(mv_b[:, i, :], st_b[:, i, :]).then_inc(mv_b_ready, 1)

            def second_norm(g, i):
                dve.wait_ge(mv_b_ready, TI * (g + 1))
                dve.wait_ge(rb_ready, g + 1)
                if not isinstance(g, int) or g > 0:
                    dve.wait_ge(t_done, NT + TI * g)
                dve.tensor_scalar(n_rows[:, i, :], x_next[:, i, :], mv_b[:, i, 0:1], rb[:, i:i + 1],
                                  ALU.subtract, ALU.mult).then_inc(n_ready, 1)

            def transposed_low(g, i):
                dve.wait_ge(t_hi, NT + TI * g + i + 1)
                dve.tensor_tensor(xt_lo[:, :, i * P:(i + 1) * P], t_bank[i % 2][:].rearrange("p (k r) -> p k r", k=K),
                                  xt_hi[:, :, i * P:(i + 1) * P].bitcast(F32), ALU.subtract).then_inc(t_lo, 1)

            def tile(h, t, norm=True, stats=True):
                tile_low(h + t // PT, t % PT)
                if norm:
                    tile_norm(h + (t + 1) // PT, (t + 1) % PT)
                if stats:
                    tile_stats(h + (t + 2) // PT, (t + 2) % PT)
                if t > 0 or h > 0:
                    tile_add(h + (t - 1) // PT, (t - 1) % PT)

            def span(h, last=False):
                for s in range(PT - LEAD if last else PT):
                    t = LEAD + s
                    tile(h, t, norm=not (last and t + 1 >= PT), stats=not (last and t + 2 >= PT))
                    if isinstance(h, int) and h == 0:
                        if s == 0:
                            mask_places()
                        if s == 1:
                            one_hots_p(0, MJ // 2)
                        if s == 2:
                            one_hots_p(MJ // 2, MJ)
                            one_hots_q()
                        if s == 3:
                            split_band()
                        if s == 4:
                            count_rows()
                        if s == 6:
                            finish_plug()
                    if s == 5:
                        scan_rows(h)
                    if s == 7:
                        add_carry(h, h_bank[0][:], cs)
                if last:
                    for i in range(TI):
                        second_stats(0, i)

            tile(0, 0)
            tile(0, 1)
            mask_positions()
            span(0)
            with dve.Fori(1, NPAIR - 1) as h:
                own.looped(h, 1, PT + R)
                span(h)
            own.left(NPAIR - 2)
            span(NPAIR - 1, last=True)
            for i in range(TI):
                second_norm(0, i)
            tile_add(NPAIR - 1, PT - 1)
            dve.wait_ge(h_used, NT)
            for i in range(TI):
                transposed_low(0, i)
            add_carry(NPAIR - 1, acc[1][:], cl)

            def group(g, scan, prep):
                for m in range(M):
                    dve.wait_ge(gelu_done, CREDIT + M * g + m + 1)
                    dve.wait_ge(h_used, NT + M * g + m - 1)
                    dve.tensor_tensor(h_lo[:, m % 2, :], g_f32[:], h_hi[:, m % 2, :].bitcast(F32),
                                      ALU.subtract).then_inc(h_split, 1)
                    if scan and m == 9:
                        scan_rows(NPAIR + g)
                    if scan and m == 12:
                        add_carry(NPAIR + g, t_bank[0][:], cl)
                    if prep and m in (10, 11):
                        for i in (2 * (m - 10), 2 * (m - 10) + 1):
                            second_stats(g + 1, i)
                    if prep and m in (13, 14):
                        for i in (2 * (m - 13), 2 * (m - 13) + 1):
                            second_norm(g + 1, i)
                if prep:
                    for i in range(TI):
                        transposed_low(g + 1, i)
                dve.wait_ge(x_cur_ready, g + 1)
                for i in range(TI):
                    if i < TI - 1:
                        dve.wait_ge(acc_done, (TI - 1) * g + i + 1)
                    else:
                        dve.wait_ge(h_used, NT + M * (g + 1))
                    dve.tensor_tensor(x_cur[:, i, :], acc[i][:], x_cur[:, i, :], ALU.add).then_inc(acc_read, 1)

            with dve.Fori(0, NB - NPAIR) as g:
                own.looped(g, 0, R + TI)
                group(g, True, True)
            own.left(NB - NPAIR)
            with dve.Fori(NB - NPAIR, NG - 1) as g:
                own.looped(g, NB - NPAIR, TI)
                group(g, False, True)
            own.left(NG - 1 - (NB - NPAIR))
            group(NG - 1, False, False)


_INS = ['x', 'ctx_2048', 'mask_BxS2_if0', 'L0_xattn_W_in', 'L0_xattn_b_in', 'L0_xattn_g_res', 'L0_xattn_g_init',
        'L0_ffn_w1', 'L0_ffn_b1', 'L0_ffn_w2', 'L0_ffn_b2']
_OUTS = [((1, S, D), 'float32')]


def kernel(**inputs):
    import numpy as _np
    import concourse.bacc as _bacc
    from concourse import mybir as _mybir
    from concourse.bass_utils import run_bass_kernel_spmd as _run

    nc = _bacc.Bacc("TRN2", target_bir_lowering=False, num_devices=1)
    arrays, args = {}, []
    for name in _INS:
        a = _np.ascontiguousarray(inputs[name])
        arrays[f"in_{name}_dram"] = a
        args.append(nc.dram_tensor(f"in_{name}_dram", a.shape, _mybir.dt.from_np(a.dtype), kind="ExternalInput").ap())
    for i, (shape, dtype) in enumerate(_OUTS):
        dt = _mybir.dt.from_np(_np.dtype(dtype))
        args.append(nc.dram_tensor(f"out_{i}_dram", shape, dt, kind="ExternalOutput").ap())
    xattn_ffn(nc, *args)
    r = _run(nc, [arrays], core_ids=[0])
    return r.results[0]["out_0_dram"]
```
